# Optimizing a Trainium2 kernel written in Bass

```python
import numpy as np
import jax
import jax.numpy as jnp

def _softmax(x, axis=-1):
    return jax.nn.softmax(x, axis=axis)

def _gelu(x):
    return jax.nn.gelu(x, approximate=True)

def _silu(x):
    return jax.nn.silu(x)

def _sigmoid(x):
    return jax.nn.sigmoid(x)

def _layernorm(x, axis=-1, eps=1e-05):
    m = jnp.mean(x, axis=axis, keepdims=True)
    v = jnp.var(x, axis=axis, keepdims=True)
    return (x - m) / jnp.sqrt(v + eps)

def _scatter_add(tgt, idx, src, axis=0):
    return tgt.at[idx].add(src)

def _segment_sum(src, seg, n):
    return jax.ops.segment_sum(src, seg, n)
kernel_name = 'mk_flamingo_gated_d2_seqx_r8_c0c386'

def setup_inputs(seed: int=0):
    np.random.seed(seed)
    _w = jnp.asarray

    def _rec_inputs():
        import jax
        import jax.numpy as jnp
        _rk = jax.random.key(seed)
        x = -7.109e-05 + 0.9999 * jax.random.normal(jax.random.fold_in(_rk, 1), (4, 256, 256), jnp.float32)
        _lenS = 256 - jax.random.randint(jax.random.fold_in(_rk, 7), (4,), 0, max(1, 256 // 4) + 1, jnp.int32)
        _lenS2 = 256 - jax.random.randint(jax.random.fold_in(_rk, 8), (4,), 0, max(1, 256 // 4) + 1, jnp.int32)
        _ctx_512P = jax.random.normal(jax.random.fold_in(_rk, 11), (4, 16, 64), jnp.float32)
        _ctx_512c = jax.random.dirichlet(jax.random.fold_in(_rk, 511), 0.3 * jnp.ones((16,), jnp.float32), (4, 256))
        _ctx_512t = jnp.einsum('bsk,bkd->bsd', _ctx_512c, _ctx_512P)
        _ctx_512t = _ctx_512t * jax.lax.rsqrt(jnp.mean(jnp.square(_ctx_512t)) + 1e-12) * 0.953939
        ctx_512 = 2.81802e-05 + 1.00001 * (_ctx_512t + 0.3 * jax.random.normal(jax.random.fold_in(_rk, 611), (4, 256, 64), jnp.float32))
        _g = jax.random.normal(jax.random.fold_in(_rk, 9001), (2, 2), jnp.float32)
        _g = jnp.sign(_g) * jnp.maximum(jnp.abs(_g), 1.0) + (_g == 0) * 1.0
        g_xattn = _g[0]
        g_ffn = _g[1]
        return (x, ctx_512, g_xattn, g_ffn)
    x, ctx_512, g_xattn, g_ffn = _rec_inputs()

    def _L0_xattn_setup():
        import jax, jax.numpy as jnp
        import numpy as np
        EPS = 1e-06
        IMAGE_DIMS = 256
        key = jax.random.key(seed)
        k1, k2, k3 = jax.random.split(key, 3)
        B, I, J, D = (16, 256, 256, 64)
        p = jax.random.normal(k1, (B, I, J), dtype=jnp.float32)
        k_v = jax.random.normal(k2, (B, J, D), dtype=jnp.float32)
        W_k = jax.random.normal(k3, (D, D), dtype=jnp.float32) * (1.0 / np.sqrt(D))
        b_k = jnp.zeros((D,), dtype=jnp.float32)
        ln_gamma = jnp.ones((J,), dtype=jnp.float32)
        ln_beta = jnp.zeros((J,), dtype=jnp.float32)
        return {'p': p, 'k_v': k_v, 'W_k': W_k, 'b_k': b_k, 'ln_gamma': ln_gamma, 'ln_beta': ln_beta}
    _L0_xattn_all = _L0_xattn_setup()
    _L0_xattn_in = {k: v for k, v in _L0_xattn_all.items() if k in ('W_k', 'b_k', 'ln_gamma', 'ln_beta')}
    del _L0_xattn_all

    def _L0_ffn_setup():
        import jax, jax.numpy as jnp
        import numpy as np
        B, S, D_IN, D_OUT, E = (4, 128, 256, 256, 32)
        MASK_DENSITY = 0.3
        THRESH = 0.5
        key = jax.random.key(seed)
        k_x, k_w, k_m, k_r = jax.random.split(key, 4)
        x = jax.random.normal(k_x, (B, S, D_IN), dtype=jnp.float32)
        bound = np.sqrt(1.0 / D_IN) * np.sqrt(3.0)
        weight = jax.random.uniform(k_w, (D_OUT, D_IN), minval=-bound, maxval=bound, dtype=jnp.float32)
        scale = jnp.ones((D_OUT,), dtype=jnp.float32)
        expert_masks = (jax.random.uniform(k_m, (E, D_OUT, D_IN)) < MASK_DENSITY).astype(jnp.float32)
        router_w = 0.01 * jax.random.normal(k_r, (E, D_IN), dtype=jnp.float32)
        return {'x': x, 'weight': weight, 'scale': scale, 'expert_masks': expert_masks, 'router_w': router_w}
    _L0_ffn_all = _L0_ffn_setup()
    _L0_ffn_in = {k: v for k, v in _L0_ffn_all.items() if k in ('weight', 'scale', 'expert_masks', 'router_w')}
    del _L0_ffn_all

    def _L1_xattn_setup():
        import jax, jax.numpy as jnp
        import numpy as np
        B, N, D = (16, 256, 64)
        H = 4
        TOP_K_RATIO = 0.3
        key = jax.random.key(seed)
        k1, k2, k3, k4 = jax.random.split(key, 4)
        h = jax.random.normal(k1, (B, N, D), dtype=jnp.float32)
        adj_raw = jax.random.uniform(k2, (B, N, N), dtype=jnp.float32)
        lim = 1.0 / np.sqrt(D)
        Wq = jax.random.uniform(k3, (D, D), minval=-lim, maxval=lim, dtype=jnp.float32)
        Wk = jax.random.uniform(k4, (D, D), minval=-lim, maxval=lim, dtype=jnp.float32)
        gamma_raw = jnp.float32(-0.85)
        return {'h': h, 'adj_raw': adj_raw, 'Wq': Wq, 'Wk': Wk, 'gamma_raw': gamma_raw}
    _L1_xattn_all = _L1_xattn_setup()
    _L1_xattn_in = {k: v for k, v in _L1_xattn_all.items() if k in ('Wq', 'Wk', 'gamma_raw')}
    del _L1_xattn_all

    def _L1_ffn_setup():
        import jax, jax.numpy as jnp
        import numpy as np
        H = 256
        E = 64
        I = 64
        SI = 64
        TOP_K = 8
        B, T = (2, 64)
        key = jax.random.key(seed)
        ks = jax.random.split(key, 8)
        s = 0.02
        return {'h': jax.random.normal(ks[0], (B, T, H), jnp.float32), 'gate_w': jax.random.normal(ks[1], (E, H), jnp.float32) * s, 'gu_w': jax.random.normal(ks[2], (E, 2 * I, H), jnp.float32) * s, 'dp_w': jax.random.normal(ks[3], (E, H, I), jnp.float32) * s, 'sh_gate_w': jax.random.normal(ks[4], (SI, H), jnp.float32) * s, 'sh_up_w': jax.random.normal(ks[5], (SI, H), jnp.float32) * s, 'sh_down_w': jax.random.normal(ks[6], (H, SI), jnp.float32) * s, 'sh_gate1_w': jax.random.normal(ks[7], (1, H), jnp.float32) * s}
    _L1_ffn_all = _L1_ffn_setup()
    _L1_ffn_in = {k: v for k, v in _L1_ffn_all.items() if k in ('gate_w', 'gu_w', 'dp_w', 'sh_gate_w', 'sh_up_w', 'sh_down_w', 'sh_gate1_w')}
    del _L1_ffn_all
    return {'x': x, 'ctx_512': ctx_512, 'g_xattn': g_xattn, 'g_ffn': g_ffn, 'L0_xattn_W_k': _L0_xattn_in['W_k'], 'L0_xattn_b_k': _L0_xattn_in['b_k'], 'L0_xattn_ln_gamma': _L0_xattn_in['ln_gamma'], 'L0_xattn_ln_beta': _L0_xattn_in['ln_beta'], 'L0_ffn_weight': _L0_ffn_in['weight'], 'L0_ffn_scale': _L0_ffn_in['scale'], 'L0_ffn_expert_masks': _L0_ffn_in['expert_masks'], 'L0_ffn_router_w': _L0_ffn_in['router_w'], 'L1_xattn_Wq': _L1_xattn_in['Wq'], 'L1_xattn_Wk': _L1_xattn_in['Wk'], 'L1_xattn_gamma_raw': _L1_xattn_in['gamma_raw'], 'L1_ffn_gate_w': _L1_ffn_in['gate_w'], 'L1_ffn_gu_w': _L1_ffn_in['gu_w'], 'L1_ffn_dp_w': _L1_ffn_in['dp_w'], 'L1_ffn_sh_gate_w': _L1_ffn_in['sh_gate_w'], 'L1_ffn_sh_up_w': _L1_ffn_in['sh_up_w'], 'L1_ffn_sh_down_w': _L1_ffn_in['sh_down_w'], 'L1_ffn_sh_gate1_w': _L1_ffn_in['sh_gate1_w']}

def reference(x, ctx_512, g_xattn, g_ffn, L0_xattn_W_k, L0_xattn_b_k, L0_xattn_ln_gamma, L0_xattn_ln_beta, L0_ffn_weight, L0_ffn_scale, L0_ffn_expert_masks, L0_ffn_router_w, L1_xattn_Wq, L1_xattn_Wk, L1_xattn_gamma_raw, L1_ffn_gate_w, L1_ffn_gu_w, L1_ffn_dp_w, L1_ffn_sh_gate_w, L1_ffn_sh_up_w, L1_ffn_sh_down_w, L1_ffn_sh_gate1_w):
    import jax
    import jax.numpy as jnp

    def _L0_xattn_ref(p, k_v, W_k, b_k, ln_gamma, ln_beta):
        import jax, jax.numpy as jnp
        import numpy as np
        EPS = 1e-06
        IMAGE_DIMS = 256
        kv = k_v @ W_k.T + b_k
        out = jnp.einsum('bij,bjd->bid', p, kv)
        scale = IMAGE_DIMS ** (-0.5)
        sim = jnp.einsum('bid,bjd->bij', out, kv) * scale
        mu = jnp.mean(sim, axis=-1, keepdims=True)
        var = jnp.var(sim, axis=-1, keepdims=True)
        sim = (sim - mu) * jax.lax.rsqrt(var + EPS) * ln_gamma + ln_beta
        attn = jax.nn.softmax(sim, axis=-1)
        return attn

    def _L0_ffn_ref(x, weight, scale, expert_masks, router_w):
        import jax, jax.numpy as jnp
        import numpy as np
        B, S, D_IN, D_OUT, E = (4, 128, 256, 256, 32)
        MASK_DENSITY = 0.3
        THRESH = 0.5
        logits = jnp.einsum('bsd,ed->bse', x, router_w)
        probs = jax.nn.softmax(logits, axis=-1)
        top1_w = jnp.max(probs, axis=-1)
        top1_idx = jnp.argmax(probs, axis=-1)
        w_q = jnp.clip(jnp.round(weight / THRESH), -1.0, 1.0)
        w_scaled = w_q * scale[:, None]
        out0 = jnp.zeros((x.shape[0], x.shape[1], weight.shape[0]), dtype=x.dtype)

        def body(out, inputs):
            e_idx, mask_e = inputs
            y = jnp.einsum('bsi,oi->bso', x, w_scaled * mask_e)
            sel = (top1_idx == e_idx)[..., None]
            out = jnp.where(sel, y * top1_w[..., None], out)
            return (out, None)
        out, _ = jax.lax.scan(body, out0, (jnp.arange(E), expert_masks))
        return out

    def _L1_xattn_ref(h, adj_raw, Wq, Wk, gamma_raw):
        import jax, jax.numpy as jnp
        import numpy as np
        B, N, D = (16, 256, 64)
        H = 4
        TOP_K_RATIO = 0.3
        b, n, dm = h.shape
        d = dm // H
        Q = (h @ Wq.T).reshape(b, n, H, d).transpose(0, 2, 1, 3)
        K = (h @ Wk.T).reshape(b, n, H, d).transpose(0, 2, 1, 3)
        sim = jnp.einsum('bhnd,bhmd->bnm', Q, K) / (jnp.sqrt(jnp.float32(d)) * H)
        k = max(1, int(n * TOP_K_RATIO))
        topk_vals = jax.lax.top_k(sim, k)[0]
        threshold = topk_vals[:, :, -1:]
        sparse_mask = (sim >= threshold).astype(sim.dtype)
        A_learned = jax.nn.sigmoid(sim) * sparse_mask
        A_learned = (A_learned + jnp.swapaxes(A_learned, -1, -2)) * 0.5
        gamma = jax.nn.sigmoid(gamma_raw)
        return (1.0 - gamma) * adj_raw + gamma * A_learned

    def _L1_ffn_ref(h, gate_w, gu_w, dp_w, sh_gate_w, sh_up_w, sh_down_w, sh_gate1_w):
        import jax, jax.numpy as jnp
        import numpy as np
        H = 256
        E = 64
        I = 64
        SI = 64
        TOP_K = 8
        B, T = (2, 64)
        Bb, Tt, Hh = h.shape
        x = h.reshape(Bb * Tt, Hh)
        N = x.shape[0]
        logits = x @ gate_w.T
        topv, topi = jax.lax.top_k(logits, TOP_K)
        rw = jax.nn.softmax(topv.astype(jnp.float32), axis=-1).astype(x.dtype)
        W = jnp.zeros((N, E), x.dtype).at[jnp.arange(N)[:, None], topi].set(rw)
        gu = jnp.einsum('nh,eih->nei', x, gu_w)
        gate, up = (gu[..., :I], gu[..., I:])
        inter = jax.nn.silu(gate) * up
        inter_w = inter * W[:, :, None]
        out = jnp.einsum('nei,ehi->nh', inter_w, dp_w)
        sh_inter = jax.nn.silu(x @ sh_gate_w.T) * (x @ sh_up_w.T)
        sh_out = sh_inter @ sh_down_w.T
        sh_g = jax.nn.sigmoid(x @ sh_gate1_w.T)
        out = out + sh_g * sh_out
        return out.reshape(Bb, Tt, Hh)
    x = x + jnp.tanh(g_xattn[0]) * _L0_xattn_ref(_layernorm(x, axis=-1), ctx_512, L0_xattn_W_k, L0_xattn_b_k, L0_xattn_ln_gamma, L0_xattn_ln_beta)
    x = x + jnp.tanh(g_ffn[0]) * _L0_ffn_ref(_layernorm(x, axis=-1), L0_ffn_weight, L0_ffn_scale, L0_ffn_expert_masks, L0_ffn_router_w)
    x = x + jnp.tanh(g_xattn[1]) * _L1_xattn_ref(ctx_512, _layernorm(x, axis=-1), L1_xattn_Wq, L1_xattn_Wk, L1_xattn_gamma_raw)
    x = x + jnp.tanh(g_ffn[1]) * _L1_ffn_ref(_layernorm(x, axis=-1), L1_ffn_gate_w, L1_ffn_gu_w, L1_ffn_dp_w, L1_ffn_sh_gate_w, L1_ffn_sh_up_w, L1_ffn_sh_down_w, L1_ffn_sh_gate1_w)
    return x

_drawn_inputs = setup_inputs


def setup_inputs(seed=0):
    import zlib

    import numpy as np

    out = dict(_drawn_inputs(seed))
    spreads = {'g_ffn': (-1.0, 0.6),
     'L0_xattn_b_k': (0.0, 2.0),
     'L0_xattn_ln_gamma': (1.0, 0.6),
     'L0_xattn_ln_beta': (0.0, 2.0),
     'L0_ffn_scale': (1.0, 0.2)}
    factors = {'L0_xattn_W_k': 8.0,
     'L1_ffn_gate_w': 7.791,
     'L1_ffn_gu_w': 6.798,
     'L1_ffn_dp_w': 6.876,
     'L1_ffn_sh_gate_w': 5.677,
     'L1_ffn_sh_up_w': 5.726,
     'L1_ffn_sh_down_w': 5.672,
     'L1_ffn_sh_gate1_w': 8.0}
    for name, (base, spread) in spreads.items():
        noise = np.random.default_rng([zlib.crc32(name.encode()), seed]).standard_normal(out[name].shape)
        drawn = base * np.exp(spread * noise) if base else spread * noise
        out[name] = jnp.asarray(drawn.astype(out[name].dtype))
    for name, factor in factors.items():
        out[name] = (out[name] * factor).astype(out[name].dtype)
    return out
```

```python
from contextlib import ExitStack

import concourse.bass as bass
from concourse import mybir

ALU = mybir.AluOpType
ACT = mybir.ActivationFunctionType
F32 = mybir.dt.float32
F16 = mybir.dt.float16
U32 = mybir.dt.uint32
AX_X = mybir.AxisListType.X

P = 128
B, S, D = 4, 256, 256
DC = 64
T = B * S // P
HT = T // 2
HN = HT * P
C = D // P
E0 = 32
GR, MB = 4, 8
BP = MB // 2
E1, I1 = 64, 64
PAIRS = E1 // 2
TOPK = int(S * 0.3)
NEG = -3.0e38
EPS = 1e-5
EPS_SIM = 1e-6
SIM_SCALE = D ** -0.5
SIM1_SCALE = 1.0 / 16.0


class Steps:

    def __init__(self, engine, sem):
        self.engine, self.sem, self.n = engine, sem, 0

    def __call__(self, instruction):
        instruction.then_inc(self.sem, 1)
        self.n += 1
        return self.n

    def need(self, step):
        self.engine.wait_ge(self.sem, step)


def flamingo_block(nc, x, ctx_t, g_xattn, g_ffn, wk_t, b_k, ln_gamma, ln_beta, w0_t, scale0, masks_t,
                   router_t, wq1_t, wk1_t, gamma_raw, gate_t, gu_t, dp_t, shg_t, shu_t, shd_t, shgate_t, out):
    with ExitStack() as stack:
        def sb(name, shape, dt=F32):
            return stack.enter_context(nc.sbuf_tensor(name, shape, dt))

        def sem(name):
            return stack.enter_context(nc.semaphore(name))

        X = sb("X", [P, T, D])
        XN = sb("XN", [P, T, D])
        Z = sb("Z", [P, T, D])
        SIM = sb("SIM", [P, T, S])
        gu16 = sb("gu16", [P, PAIRS, 2, C, 256], F16)
        m16 = gu16[:, PAIRS // 2:, :, :, :].rearrange("p a b c d -> p (a b c d)").rearrange(
            "p (c e o) -> p c e o", c=C, e=E0)
        stage_dp = sb("stage_dp", [P, 2 * C * GR * 2 * D])
        mask_stage = stage_dp[:, :].rearrange("p (s c a n) -> p s c a n", s=2, c=C, a=GR)
        dp16 = stage_dp[:, :].bitcast(F16).rearrange("p (q s n) -> p q s n", q=PAIRS, s=2)
        xg = sb("xg", [P, T, 2, C, GR * P], F16)
        act_area = xg[:, :, :, :, :].rearrange("p a b c d -> p (a b c d)")
        silu = act_area[:, 0:2048].bitcast(F32).rearrange("p (s n) -> p s n", s=2)
        gated = act_area[:, 2048:4096].bitcast(F32).rearrange("p (s n) -> p s n", s=2)
        inter = act_area[:, 4096:6144].bitcast(F32).rearrange("p (s n) -> p s n", s=2)
        inter16 = act_area[:, 6144:8192].rearrange("p (s h n) -> p s h n", s=2, h=2)
        stage = sb("stage", [P, 2, 768])
        area = stage[:, :, :].rearrange("p s n -> p (s n)").bitcast(F16)
        rows16 = area[:, 0:2048].rearrange("p (r h n) -> p r h n", r=4, h=2)
        diag = area[:, 2048:3072].rearrange("p (r a n) -> p r a n", r=2, a=GR)
        early = sb("early", [P, 5120])
        ctx_sb = early[0:DC + 1, 0:1024]
        kv_t = early[0:DC, 1024:2048]
        kv = early[:, 2048:2560].rearrange("p (t d) -> p t d", d=DC)
        q_t = early[0:DC, 2560:3072]
        k_t = early[0:DC, 3072:3584]
        p_t = early[:, 3584:4608].rearrange("p (s c n) -> p s c n", s=2, c=C)
        o_t = early[0:DC, 4608:5120].rearrange("p (s n) -> p s n", s=2)
        late = early[:, :].bitcast(F16)
        x16 = late[:, 0:4096].rearrange("p (h s c n) -> p h s c n", h=2, s=2, c=C)
        pick = late[:, 4096:8192]
        w_t = late[:, 8192:9216].rearrange("p (h n) -> p h n", h=2)
        ws_t = late[0:2, 9216:10240].rearrange("p (h n) -> p h n", h=2)

        xn_t = sb("xn_t", [P, 2, C, P])
        gamma_sb = sb("gamma_sb", [P, S])
        beta_sb = sb("beta_sb", [P, S])
        scale_sb = sb("scale_sb", [P, D])
        ident = sb("ident", [P, P])
        ident16 = sb("ident16", [P, P], F16)
        iota = sb("iota", [P, E0])
        minus_half = sb("minus_half", [P, 4])
        wk_sb = sb("wk_sb", [DC + 1, DC])
        wq1_sb = sb("wq1_sb", [DC, DC])
        wk1_sb = sb("wk1_sb", [DC, DC])
        x3_t = sb("x3_t", [P, 2, C, 2 * P])
        w0_sb, tern = x3_t[:, 0, :, :], x3_t[:, 1, :, :]
        router_sb = sb("router_sb", [P, C, E0])
        gate_sb = sb("gate_sb", [P, C, E1 + 1])
        gates = sb("gates", [P, 5])
        tg = sb("tg", [P, 5])
        k_mix = sb("k_mix", [P, 4])
        shared_stage = sb("shared_stage", [P, C, 128])
        shared16 = sb("shared16", [P, 2, C, 128], F16)
        shared_dn_stage = sb("shared_dn_stage", [I1, D])
        shared_dn16 = sb("shared_dn16", [I1, 2, D], F16)
        bn = sb("bn", [P, T, 6])
        mv = sb("mv", [P, T, 2])
        NR = 3 * B + 4
        var_in = sb("var_in", [P, NR, 4])
        rstd = sb("rstd", [P, NR, 4])
        tiny = sb("tiny", [P, 8, T])
        c_mem = sb("c_mem", [P, T, MB])
        oh = sb("oh", [P, 2, E0])
        ohw = sb("ohw", [P, 2, E0])
        ex0 = sb("ex0", [P, E0])
        lg0 = sb("lg0", [P, 2, E0])
        grp = sb("grp", [P, 2, GR])
        m8 = sb("m8", [P, 2, 8])
        m8i = sb("m8i", [P, 2, 8], U32)
        idxf = sb("idxf", [P, 2])
        work = sb("work", [P, S])
        t8 = sb("t8", [P, 8])
        th1 = sb("th1", [P, S])
        lg = sb("lg", [P, HT, E1 + 1])
        rep = Z[:, 0, :].rearrange("p (t n) -> p t n", t=HT)
        ex1 = Z[:, 1, :].rearrange("p (t n) -> p t n", t=HT)
        w16 = Z[:, 2, :].bitcast(F16).rearrange("p (t n) -> p t n", t=HT)
        top = sb("top", [P, HT, 8])
        ws16 = sb("ws16", [P, HT, 2], F16)
        ones2 = sb("ones2", [2, I1], F16)
        nmax, den, rden, r16, nm0, wtop, den1, sgt = (tiny[:, j, :] for j in range(8))

        bank = [stack.enter_context(nc.psum_tensor(f"bank{j}", [P, 512], F32)) for j in range(8)]
        ps_kv = [bank[0], bank[7]]
        ps_tr = [bank[1], bank[5]]
        ps_small = [bank[2], bank[6]]
        ps_sim = [bank[3], bank[4]]
        ps_y = [bank[3], bank[4], bank[5], bank[6]]
        ps_gate = [bank[3], bank[4]]
        ps_up = [bank[5], bank[6]]
        ps_w = bank[1]
        ps_prep = bank[2]
        ps_down = [bank[0], bank[7]]

        x_in = [sem(f"x_in{b}") for b in range(B)]
        ctx_in, attn_in, small_in = sem("ctx_in"), sem("attn_in"), sem("small_in")
        mask_in = [sem(f"mask_in{s}") for s in range(2)]
        stage_in = [sem(f"stage_in{s}") for s in range(2)]
        ones_set, const_set, tern_set = sem("ones_set"), sem("const_set"), sem("tern_set")
        pool_step, dve_step, act_step = sem("pool_step"), sem("dve_step"), sem("act_step")
        gates_done = sem("gates_done")
        var_ready, rstd_ready = sem("var_ready"), sem("rstd_ready")
        mask_ready = sem("mask_ready")
        proj_ready, proj_copied = sem("proj_ready"), sem("proj_copied")
        p_ready, pt_ready, pt_copied = sem("p_ready"), sem("pt_ready"), sem("pt_copied")
        o_ready, o_copied, sim_ready = sem("o_ready"), sem("o_copied"), sem("sim_ready")
        sim_used, z_ready, exp_ready = sem("sim_used"), sem("z_ready"), sem("exp_ready")
        sim1_ready, sim1_copied = sem("sim1_ready"), sem("sim1_copied")
        xn_ready, xnt_ready, xnt_copied = sem("xn_ready"), sem("xnt_ready"), sem("xnt_copied")
        logits_ready, max_ready, exp0_ready = sem("logits_ready"), sem("max_ready"), sem("exp0_ready")
        diag_ready, xg_ready, xg_copied = sem("diag_ready"), sem("xg_ready"), sem("xg_copied")
        y_ready, y_free = sem("y_ready"), sem("y_free")
        th_ready, adj_ready, sym_ready = sem("th_ready"), sem("adj_ready"), sem("sym_ready")
        hi_ready, lo_ready = sem("hi_ready"), sem("lo_ready")
        xn3_ready, x3t_ready, x3t_copied = sem("xn3_ready"), sem("x3t_ready"), sem("x3t_copied")
        x16hi_ready, x16_ready = sem("x16hi_ready"), sem("x16_ready")
        logits1_ready, top_ready, exp1_ready = sem("logits1_ready"), sem("top_ready"), sem("exp1_ready")
        w16_ready, wt_ready, wt_copied = sem("w16_ready"), sem("wt_ready"), sem("wt_copied")
        pick_set, shared_hi, shared_set = sem("pick_set"), sem("shared_hi"), sem("shared_set")
        gate_ready, up_ready, wb_ready = sem("gate_ready"), sem("up_ready"), sem("wb_ready")
        silu_ready, gated_ready, inter_ready = sem("silu_ready"), sem("gated_ready"), sem("inter_ready")
        ihi_ready, ilo_ready = sem("ihi_ready"), sem("ilo_ready")
        down_ready = sem("down_ready")
        out_ready, out_done = sem("out_ready"), sem("out_done")
        ones2_set, logits1_copied, sym_added = (
            sem("ones2_set"), sem("logits1_copied"), sem("sym_added"))

        x_d = x.rearrange("b s d -> (b s) d").rearrange("(t p) d -> p t d", p=P)
        out_d = out.rearrange("b s d -> (b s) d").rearrange("(t p) d -> p t d", p=P)
        mask_d = masks_t.rearrange("(c p) (a m) n -> p c a m n", p=P, a=GR)
        gu_d = gu_t.rearrange("(c p) q n -> p c q n", p=P)
        dp_d = dp_t.rearrange("(q p) n -> p q n", p=P)
        stage_gu = [stage[:, s, 0:512].rearrange("p (c n) -> p c n", c=C) for s in range(2)]
        stage_dn = [stage[:, s, 512:768] for s in range(2)]
        SMALL = 16 * 16

        block = stack.enter_context(nc.Block())

        @block.sync
        def _(sp):
            for b in range(B):
                sp.dma_start(X[:, 2 * b:2 * b + 2, :], x_d[:, 2 * b:2 * b + 2, :]).then_inc(x_in[b], 16)
            for bp in range(BP):
                if bp >= 2:
                    sp.wait_ge(mask_ready, C * GR * (bp - 1))
                for c in range(C):
                    sp.dma_start(mask_stage[:, bp % 2, c, :, :],
                                 mask_d[:, c, :, bp, :]).then_inc(mask_in[bp % 2], 16)

            def load_pair(q, s):
                sp.dma_start(stage_gu[s], gu_d[:, :, bass.ds(q, 1), :].rearrange("p c q n -> p c (q n)")
                             ).then_inc(stage_in[s], 16)
                sp.dma_start(stage_dn[s], dp_d[:, bass.ds(q, 1), :].rearrange("p q n -> p (q n)")
                             ).then_inc(stage_in[s], 16)

            sp.wait_ge(xg_ready, T)
            load_pair(0, 0)
            load_pair(1, 1)
            with sp.Fori(0, (PAIRS - 2) // 2) as turn:
                q = turn * 2 + 2
                for s in range(2):
                    sp.wait_ge(lo_ready, q + (s - 1))
                    load_pair(q + s, s)
            for t in range(T):
                sp.wait_ge(out_ready, t + 1)
                sp.dma_start(out_d[:, t, :], X[:, t, :]).then_inc(out_done, 16)
            sp.wait_ge(out_done, 16 * T)

        @block.gpsimd
        def _(pool):
            steps = Steps(pool, pool_step)
            nc.gpsimd.memset(ctx_sb[DC:DC + 1, :], 1.0).then_inc(ones_set, 1)
            pool.wait_ge(ones_set, 1)
            nc.gpsimd.memset(minus_half[:, :], -0.5).then_inc(const_set, 1)
            a = steps(nc.gpsimd.memset(ident[:, :], 0.0))
            b16 = steps(nc.gpsimd.memset(ident16[:, :], 0.0))
            for ready, m in ((a, ident), (b16, ident16)):
                steps.need(ready)
                nc.gpsimd.affine_select(out=m[:, :], in_=m[:, :], compare_op=ALU.not_equal, fill=1.0, base=0,
                                        pattern=[[-1, P]], channel_multiplier=1).then_inc(const_set, 1)
            nc.gpsimd.iota(iota[:, :], pattern=[[1, E0]], base=0, channel_multiplier=0,
                           allow_small_or_imprecise_dtypes=True).then_inc(const_set, 1)
            pool.wait_ge(const_set, 1)

            def rsqrt(r, n):
                pool.wait_ge(var_ready, r + 1)
                nc.gpsimd.tensor_tensor(rstd[:, r, 0:n], var_in[:, r, 0:n], minus_half[:, 0:n],
                                        ALU.pow).then_inc(rstd_ready, 1)

            def mask_piece(n):
                bp, c, g = n // (C * GR), n // GR % C, n % GR
                if n == 0:
                    pool.wait_ge(tern_set, 1)
                if n % (C * GR) == 0:
                    pool.wait_ge(mask_in[bp % 2], 16 * C * (bp // 2 + 1))
                e = g * MB + 2 * bp
                for m in range(2):
                    last = nc.gpsimd.tensor_tensor(m16[:, c, e + m, :], mask_stage[:, bp % 2, c, g, m * D:(m + 1) * D],
                                                   tern[:, c, :], ALU.mult)
                last.then_inc(mask_ready, 1)

            pieces = C * GR * BP
            done = 0
            for r in range(3 * B):
                rsqrt(r, 2)
                upto = pieces * (r + 1) // (3 * B) if r >= 2 else 0
                for n in range(done, upto):
                    mask_piece(n)
                done = max(done, upto)
            pool.wait_ge(shared_hi, 2)
            nc.gpsimd.tensor_tensor(shared16[:, 1, :, :], shared_stage[:, :, :], shared16[:, 0, :, :],
                                    ALU.subtract).then_inc(shared_set, 1)
            nc.gpsimd.tensor_tensor(shared_dn16[:, 1, :], shared_dn_stage[:, :], shared_dn16[:, 0, :],
                                    ALU.subtract).then_inc(shared_set, 1)
            pool.wait_ge(xg_ready, T)
            pool.wait_ge(sim1_ready, B)
            pool.wait_ge(sim_ready, B)
            a = steps(nc.gpsimd.memset(pick, 0.0))
            pick3 = pick.rearrange("p (e j) -> p e j", e=E1)
            steps.need(a)
            for base in (0, -E1):
                nc.gpsimd.affine_select(out=pick3, in_=pick3, compare_op=ALU.not_equal, fill=1.0, base=base,
                                        pattern=[[-1, E1], [0, I1]], channel_multiplier=1).then_inc(pick_set, 1)
                pool.wait_ge(pick_set, 1)

            def low_half(q, s):
                pool.wait_ge(hi_ready, q + 1)
                nc.gpsimd.tensor_tensor(gu16[:, bass.ds(q, 1), 1, :, :].rearrange("p q c n -> p (q c) n"),
                                        stage_gu[s], gu16[:, bass.ds(q, 1), 0, :, :].rearrange("p q c n -> p (q c) n"),
                                        ALU.subtract)
                nc.gpsimd.tensor_tensor(dp16[:, bass.ds(q, 1), 1, :].rearrange("p q n -> p (q n)"), stage_dn[s],
                                        dp16[:, bass.ds(q, 1), 0, :].rearrange("p q n -> p (q n)"),
                                        ALU.subtract).then_inc(lo_ready, 1)

            with pool.Fori(0, (PAIRS // 2 - 0) // 2) as turn:
                q = turn * 2 + 0
                for s in range(2):
                    low_half(q + s, s)
            for r in range(3 * B, 3 * B + 4):
                rsqrt(r, HT)
            with pool.Fori(0, (PAIRS - PAIRS // 2) // 2) as turn:
                q = turn * 2 + PAIRS // 2
                for s in range(2):
                    low_half(q + s, s)

        @block.scalar
        def _(act):
            def copy(dst, src, scale=1.0):
                return nc.scalar.activation(dst, src, ACT.Copy, scale=scale)

            act.dma_start(ctx_sb[0:DC, :], ctx_t).then_inc(ctx_in, 16)
            act.dma_start(wk_sb[0:DC, :], wk_t).then_inc(attn_in, 16)
            act.dma_start(wk_sb[DC:DC + 1, :], b_k.rearrange("(a d) -> a d", a=1)).then_inc(attn_in, 16)
            act.dma_start(w0_sb[:, :, :], w0_t.rearrange("(c p) n -> p c n", p=P)).then_inc(small_in, 16)
            for dst, src in ((gamma_sb, ln_gamma), (beta_sb, ln_beta), (scale_sb, scale0),
                             (gates[:, 0:2], g_xattn), (gates[:, 2:4], g_ffn), (gates[:, 4:5], gamma_raw)):
                act.dma_start(dst if dst.shape[-1] < 8 else dst[:, :],
                              src.rearrange("(a d) -> a d", a=1).to_broadcast([P, src.shape[0]])).then_inc(small_in, 16)
            act.dma_start(wq1_sb[:, :], wq1_t).then_inc(small_in, 16)
            act.dma_start(wk1_sb[:, :], wk1_t).then_inc(small_in, 16)
            act.dma_start(router_sb[:, :, :], router_t.rearrange("(c p) n -> p c n", p=P)).then_inc(small_in, 16)
            act.dma_start(gate_sb[:, :, 0:E1], gate_t.rearrange("(c p) n -> p c n", p=P)).then_inc(small_in, 16)
            act.dma_start(gate_sb[:, 0, E1:E1 + 1], shgate_t[0:P, :]).then_inc(small_in, 16)
            act.dma_start(gate_sb[:, 1, E1:E1 + 1], shgate_t[P:D, :]).then_inc(small_in, 16)
            act.dma_start(shared_stage[:, :, 0:I1], shg_t.rearrange("(c p) n -> p c n", p=P)).then_inc(small_in, 16)
            act.dma_start(shared_stage[:, :, I1:128], shu_t.rearrange("(c p) n -> p c n", p=P)).then_inc(small_in, 16)
            act.dma_start(shared_dn_stage[:, :], shd_t).then_inc(small_in, 16)

            for h in range(2):
                act.wait_ge(proj_ready, h + 1)
                copy(kv_t[:, h * 512:(h + 1) * 512], ps_kv[h][0:DC, :]).then_inc(proj_copied, 1)
            act.wait_ge(proj_ready, 3)
            copy(kv[:, :, :].rearrange("p t d -> p (t d)"), ps_small[0][:, :]).then_inc(proj_copied, 1)
            act.wait_ge(small_in, SMALL)
            nc.scalar.activation(tg[:, 0:4], gates[:, 0:4], ACT.Tanh).then_inc(act_step, 1)
            nc.scalar.activation(tg[:, 4:5], gates[:, 4:5], ACT.Tanh, scale=0.5).then_inc(gates_done, 1)

            def softmax_rows(b):
                for t in (2 * b, 2 * b + 1):
                    act.wait_ge(z_ready, t + 1)
                    nc.scalar.activation(Z[:, t, :], Z[:, t, :], ACT.Exp, bias=nmax[:, t:t + 1],
                                         accum_out=den[:, t:t + 1]).then_inc(exp_ready, 1)

            for b in range(B):
                act.wait_ge(pt_ready, b + 1)
                if b >= 2:
                    act.wait_ge(o_ready, b - 1)
                copy(p_t[:, b % 2, :, :].rearrange("p c n -> p (c n)"), ps_tr[b % 2][:, :]).then_inc(pt_copied, 1)
                act.wait_ge(o_ready, b + 1)
                if b >= 2:
                    act.wait_ge(sim_ready, b - 1)
                copy(o_t[:, b % 2, :], ps_small[b % 2][0:DC, 0:256]).then_inc(o_copied, 1)
                if b >= 1:
                    softmax_rows(b - 1)
            for h in range(2):
                for j, dst in enumerate((q_t, k_t)):
                    act.wait_ge(proj_ready, 4 + 2 * h + j)
                    copy(dst, ps_kv[j][0:DC, :]).then_inc(proj_copied, 1)
                for k in range(2):
                    act.wait_ge(sim1_ready, 2 * h + k + 1)
                    t = 4 * h + 2 * k
                    copy(SIM[:, t:t + 2, :].rearrange("p t n -> p (t n)"), ps_kv[k][:, :],
                         SIM1_SCALE).then_inc(sim1_copied, 1)
                if h == 0:
                    softmax_rows(B - 1)

            def route0(t):
                act.wait_ge(xnt_ready, t + 1)
                copy(xn_t[:, t % 2, :, :].rearrange("p c n -> p (c n)"), ps_tr[t % 2][:, 0:256]).then_inc(xnt_copied, 1)
                act.wait_ge(max_ready, t + 1)
                nc.scalar.activation(ex0[:, :], lg0[:, t % 2, :], ACT.Exp, bias=nm0[:, t:t + 1],
                                     accum_out=den1[:, t:t + 1]).then_inc(exp0_ready, 1)

            def grouped(t):
                for n in range(2 * C):
                    act.wait_ge(xg_ready, t + 1)
                    copy(xg[:, t, n // C, n % C, :], ps_grp[n][:, :]).then_inc(xg_copied, 1)

            ps_grp = [bank[0], bank[7], bank[3], bank[4]]
            for t in range(T + 1):
                if t < T:
                    route0(t)
                if t >= 1:
                    grouped(t - 1)

            copy(shared16[:, 0, :, :], shared_stage[:, :, :]).then_inc(shared_hi, 1)
            copy(shared_dn16[:, 0, :], shared_dn_stage[:, :]).then_inc(shared_hi, 1)

            def tanh_row(t):
                if t >= 1:
                    act.wait_ge(adj_ready, t)
                steps_t = nc.scalar.activation(th1[:, :], SIM[:, bass.ds(t, 1), :].rearrange("p t n -> p (t n)"),
                                               ACT.Tanh, scale=0.5)
                steps_t.then_inc(act_step, 1)
                act.wait_ge(act_step, t + 2)
                nc.scalar.activation(th1[:, :], th1[:, :], ACT.Copy, bias=1.0).then_inc(th_ready, 1)

            def high_half(q, s, turn):
                act.wait_ge(stage_in[s], turn)
                copy(gu16[:, bass.ds(q, 1), 0, :, :].rearrange("p q c n -> p (q c) n"), stage_gu[s])
                copy(dp16[:, bass.ds(q, 1), 0, :].rearrange("p q n -> p (q n)"), stage_dn[s]).then_inc(hi_ready, 1)

            act.wait_ge(mask_ready, C * GR * BP)
            for bp in range(BP):
                tanh_row(bp)
                for j in range(4):
                    high_half(bp * 4 + j, j % 2, bp * 64 + 32 * (j // 2 + 1))

            def prep_rows(h):
                for u in (2 * h, 2 * h + 1):
                    act.wait_ge(x3t_ready, u + 1)
                    if u >= 2:
                        act.wait_ge(x16_ready, u - 1)
                        act.wait_ge(logits1_ready, 2 * u - 2)
                    copy(x3_t[:, u % 2, :, :].rearrange("p c n -> p (c n)"), ps_prep[:, :]).then_inc(x3t_copied, 1)
                    act.wait_ge(x3t_copied, u + 1)
                    copy(x16[:, h, 0, :, (u % 2) * 256:(u % 2 + 1) * 256], x3_t[:, u % 2, :, :]).then_inc(x16hi_ready, 1)
                for t in range(4 * h, 4 * h + 4):
                    act.wait_ge(top_ready, t + 1)
                    nc.scalar.activation(ex1[:, t % HT, :], lg[:, t % HT, 0:E1], ACT.Exp, bias=nmax[:, t:t + 1])
                    nc.scalar.activation(sgt[:, t:t + 1], lg[:, t % HT, E1:E1 + 1], ACT.Tanh,
                                         scale=0.5).then_inc(exp1_ready, 1)

            def prep_weights(h):
                act.wait_ge(wt_ready, h + 1)
                copy(w_t[:, h, :], ps_prep[:, :])
                copy(ws_t[:, h, :], ps_w[0:2, :]).then_inc(wt_copied, 1)

            tanh_row(4)
            tanh_row(5)
            tanh_row(6)
            prep_rows(0)
            tanh_row(7)
            prep_weights(0)

            NS = PAIRS + 1

            def silu_step(n, s, m=P):
                act.wait_ge(gate_ready, n + 1)
                act.wait_ge(gated_ready, n - 1)
                nc.scalar.activation(silu[0:m, s, :], ps_gate[s][0:m, :], ACT.Silu).then_inc(silu_ready, 1)

            def high_step(n, s, m=P):
                act.wait_ge(inter_ready, n + 1)
                act.wait_ge(down_ready, n - 1)
                copy(inter16[0:m, s, 0, :], inter[0:m, s, :]).then_inc(ihi_ready, 1)

            for h in range(2):
                b0 = h * NS
                for n in (0, 1):
                    s = (n + 1) % 2
                    act.wait_ge(gate_ready, b0 + n + 1)
                    if b0 + n >= 2:
                        act.wait_ge(gated_ready, b0 + n - 1)
                    m = I1 if n == 0 else P
                    nc.scalar.activation(silu[0:m, s, :], ps_gate[s][0:m, :], ACT.Silu).then_inc(silu_ready, 1)
                    act.wait_ge(inter_ready, b0 + n + 1)
                    if b0 + n >= 2:
                        act.wait_ge(down_ready, b0 + n - 1)
                    copy(inter16[0:m, s, 0, :], inter[0:m, s, :]).then_inc(ihi_ready, 1)
                if h == 0:
                    with act.Fori(0, (15 - 1) // 2) as turn:
                        q = turn * 2 + 1
                        for j in range(2):
                            silu_step(q + (1 + j), (1 + j) % 2)
                            high_half(q + (15 + j), j % 2, (q + (15 + j) - j) * 16 + 32)
                            high_step(q + (1 + j), (1 + j) % 2)
                    high_half(30, 0, 32 * 16)
                    high_half(31, 1, 32 * 16)
                    prep_rows(1)
                    prep_weights(1)
                    with act.Fori(0, (31 - 15) // 2) as turn:
                        q = turn * 2 + 15
                        for j in range(2):
                            silu_step(q + (1 + j), (1 + j) % 2)
                            high_step(q + (1 + j), (1 + j) % 2)
                else:
                    with act.Fori(0, (31 - 1) // 2) as turn:
                        q = turn * 2 + 1
                        for j in range(2):
                            silu_step(q + (b0 + 1 + j), (1 + j) % 2)
                            high_step(q + (b0 + 1 + j), (1 + j) % 2)
                silu_step(b0 + 32, 1)
                high_step(b0 + 32, 1)

        @block.tensor
        def _(pe):
            mm = nc.tensor.matmul

            pe.wait_ge(ones_set, 1)
            pe.wait_ge(ctx_in, 16)
            pe.wait_ge(attn_in, 32)
            for h in range(2):
                mm(ps_kv[h][0:DC, :], wk_sb[:, :], ctx_sb[:, h * 512:(h + 1) * 512], start=True, stop=True
                   ).then_inc(proj_ready, 1)
            for t in range(T):
                last = mm(ps_small[0][:, t * DC:(t + 1) * DC], ctx_sb[:, t * P:(t + 1) * P], wk_sb[:, :],
                          start=True, stop=True)
            last.then_inc(proj_ready, 1)
            pe.wait_ge(const_set, 4)

            def transpose_p(b):
                pe.wait_ge(p_ready, 2 * b + 2)
                if b >= 2:
                    pe.wait_ge(pt_copied, b - 1)
                for c in range(C):
                    for k in range(2):
                        last = nc.tensor.transpose(ps_tr[b % 2][:, c * 256 + k * P:c * 256 + (k + 1) * P],
                                                   XN[:, 2 * b + k, c * P:(c + 1) * P], ident[:, :])
                last.then_inc(pt_ready, 1)

            def out_and_sim(b):
                pe.wait_ge(pt_copied, b + 1)
                pe.wait_ge(proj_copied, 3)
                if b >= 2:
                    pe.wait_ge(o_copied, b - 1)
                for c in range(C):
                    last = mm(ps_small[b % 2][0:DC, 0:256], kv[:, 2 * b + c, :], p_t[:, b % 2, c, :],
                              start=(c == 0), stop=(c == C - 1))
                last.then_inc(o_ready, 1)
                pe.wait_ge(o_copied, b + 1)
                if b >= 2:
                    pe.wait_ge(sim_used, 2 * (b - 1))
                for k in range(2):
                    last = mm(ps_sim[b % 2][:, k * 256:(k + 1) * 256], o_t[:, b % 2, k * P:(k + 1) * P],
                              kv_t[:, b * S:(b + 1) * S], start=True, stop=True)
                last.then_inc(sim_ready, 1)

            transpose_p(0)
            for b in range(B):
                if b + 1 < B:
                    transpose_p(b + 1)
                out_and_sim(b)

            pe.wait_ge(small_in, SMALL)
            for h in range(2):
                for j, w in enumerate((wq1_sb, wk1_sb)):
                    if h == 1:
                        pe.wait_ge(sim1_copied, j + 1)
                    mm(ps_kv[j][0:DC, :], w[:, :], ctx_sb[0:DC, h * 512:(h + 1) * 512], start=True, stop=True
                       ).then_inc(proj_ready, 1)
                for k in range(2):
                    pe.wait_ge(proj_copied, 5 + 2 * h)
                    for i in range(2):
                        last = mm(ps_kv[k][:, i * 256:(i + 1) * 256], q_t[:, k * S + i * P:k * S + (i + 1) * P],
                                  k_t[:, k * S:(k + 1) * S], start=True, stop=True)
                    last.then_inc(sim1_ready, 1)

            def router(t):
                pe.wait_ge(xn_ready, t + 1)
                if t == 0:
                    pe.wait_ge(pt_copied, B)
                if t >= 2:
                    pe.wait_ge(xnt_copied, t - 1)
                for c in range(C):
                    last = nc.tensor.transpose(ps_tr[t % 2][:, c * P:(c + 1) * P], XN[:, t, c * P:(c + 1) * P],
                                               ident[:, :])
                last.then_inc(xnt_ready, 1)
                pe.wait_ge(xnt_copied, t + 1)
                if t >= 2:
                    pe.wait_ge(max_ready, t - 1)
                for c in range(C):
                    last = mm(ps_small[t % 2][:, 256:256 + E0], xn_t[:, t % 2, c, :], router_sb[:, c, :],
                              start=(c == 0), stop=(c == C - 1))
                last.then_inc(logits_ready, 1)

            ps_grp = [bank[0], bank[7], bank[3], bank[4]]

            def group_rows(t):
                pe.wait_ge(diag_ready, t + 1)
                if t == 0:
                    pe.wait_ge(sim1_copied, B)
                    pe.wait_ge(sim_used, T)
                else:
                    pe.wait_ge(xg_copied, 2 * C * t)
                for n in range(2 * C):
                    last = mm(ps_grp[n][:, :], rows16[:, t % 4, n // C, (n % C) * P:(n % C + 1) * P],
                              diag[:, t % 2, :, :].rearrange("p a n -> p (a n)"), start=True, stop=True)
                last.then_inc(xg_ready, 1)

            for t in range(T + 1):
                if t < T:
                    router(t)
                if t >= 1:
                    group_rows(t - 1)

            def experts0(h, bp, first):
                pe.wait_ge(mask_ready, bp * (C * GR) + C * GR if h == 0 else C * GR * BP)
                for k in range(HT):
                    pe.wait_ge(y_free, bp * HT + (h * BP * HT + k + 1))
                    n = 0
                    for s in range(2):
                        for c in range(C):
                            for g in range(GR):
                                last = mm(ps_y[k][:, :], xg[:, HT * h + k, s, c, g * P:(g + 1) * P],
                                          m16[:, c, bass.ds(bp * 2 + g * MB, 2), :].rearrange("p e o -> p (e o)"),
                                          start=(n == 0), stop=(n == 2 * C * GR - 1))
                                n += 1
                    last.then_inc(y_ready, 1)

            def symmetric(h):
                for k in range(2):
                    pe.wait_ge(adj_ready, 4 * h + 2 * k + 2)
                    dst = (bank[0], bank[1])[k]
                    for i in range(2):
                        for j in range(2):
                            last = nc.tensor.transpose(dst[:, i * 256 + j * P:i * 256 + (j + 1) * P],
                                                       SIM[:, 4 * h + 2 * k + j, i * P:(i + 1) * P], ident[:, :])
                    last.then_inc(sym_ready, 1)

            def prep_logits(h):
                if h == 0:
                    pe.wait_ge(sym_added, 2)
                else:
                    pe.wait_ge(inter_ready, 16)
                for u in (2 * h, 2 * h + 1):
                    pe.wait_ge(xn3_ready, 2 * u + 2)
                    if u >= 1:
                        pe.wait_ge(x3t_copied, u)
                    for c in range(C):
                        for k in range(2):
                            last = nc.tensor.transpose(ps_prep[:, c * 256 + k * P:c * 256 + (k + 1) * P],
                                                       XN[:, 2 * u + k, c * P:(c + 1) * P], ident[:, :])
                    last.then_inc(x3t_ready, 1)
                    pe.wait_ge(x3t_copied, u + 1)
                    for k in range(2):
                        j = (u % 2) * 2 + k
                        for c in range(C):
                            last = mm(ps_w[:, j * 80:j * 80 + E1 + 1], x3_t[:, u % 2, c, k * P:(k + 1) * P],
                                      gate_sb[:, c, :], start=(c == 0), stop=(c == C - 1))
                        last.then_inc(logits1_ready, 1)

            def prep_wt(h):
                pe.wait_ge(w16_ready, HT * h + HT)
                if h == 0:
                    pe.wait_ge(sym_added, 4)
                for k in range(HT):
                    mm(ps_prep[:, k * P:(k + 1) * P], w16[:, k, :], ident16[:, :], start=True, stop=True)
                    last = mm(ps_w[0:2, k * P:(k + 1) * P], ws16[:, k, :], ident16[:, :], start=True, stop=True)
                last.then_inc(wt_ready, 1)

            pe.wait_ge(xg_copied, 2 * C * T)
            with pe.Fori(0, BP) as bp:
                experts0(0, bp, True)
            experts0(1, 0, False)
            symmetric(0)
            with pe.Fori(1, 3) as bp:
                experts0(1, bp, False)
            prep_logits(0)
            experts0(1, 3, False)
            pe.wait_ge(sym_added, 2)
            symmetric(1)
            prep_wt(0)

            NS = PAIRS + 1
            SPLIT = ((0, 0), (0, 1), (1, 0))

            def project(n, s, q, h, m=P):
                pe.wait_ge(inter_ready, n)
                if q is None:
                    mm(ps_w[0:m, :], ones2[:, :], ws_t[:, h, :], start=True, stop=True).then_inc(wb_ready, 1)
                else:
                    mm(ps_w[:, :], pick[:, bass.ds(q * P, P)], w_t[:, h, :], start=True, stop=True
                       ).then_inc(wb_ready, 1)
                for part, (dst, ready) in enumerate(((ps_gate[s], gate_ready), (ps_up[s], up_ready))):
                    k = 0
                    for a, b in SPLIT:
                        for c in range(C):
                            if q is None:
                                w = shared16[:, a, c, part * I1:(part + 1) * I1]
                            else:
                                w = gu16[:, bass.ds(q, 1), a, c, part * P:(part + 1) * P].rearrange("p q n -> p (q n)")
                            last = mm(dst[0:m, :], w, x16[:, h, b, c, :], start=(k == 0), stop=(k == 3 * C - 1))
                            k += 1
                    last.then_inc(ready, 1)

            def down(n, s, q, m=P):
                pe.wait_ge(ilo_ready, n + 1)
                for k in range(HT):
                    dst = ps_down[k // 2][:, (k % 2) * D:(k % 2 + 1) * D]
                    for j, (a, b) in enumerate(SPLIT):
                        if q is None:
                            w = shared_dn16[:, b, :]
                        else:
                            w = dp16[:, bass.ds(q, 1), b, :].rearrange("p q n -> p (q n)")
                        last = mm(dst, inter16[0:m, s, a, k * P:(k + 1) * P], w,
                                  start=(q is None and j == 0 and k % 2 == 0), stop=True, skip_group_check=True)
                last.then_inc(down_ready, 1)

            def slots_free(n):
                pe.wait_ge(silu_ready, n - 1)
                pe.wait_ge(gated_ready, n - 1)

            pe.wait_ge(pick_set, 2)
            pe.wait_ge(ones2_set, 1)
            pe.wait_ge(shared_set, 2)
            for h in range(2):
                b0 = h * NS
                pe.wait_ge(wt_copied, h + 1)
                pe.wait_ge(x16_ready, 2 * h + 2)
                if h == 0:
                    pe.wait_ge(y_free, HT + 2 * BP * HT)
                    pe.wait_ge(sym_added, 4)
                else:
                    slots_free(b0)
                project(b0, 1, None, h, I1)
                if h == 1:
                    slots_free(b0 + 1)
                pe.wait_ge(lo_ready, 1)
                project(b0 + 1, 0, 0, h)
                if h == 1:
                    pe.wait_ge(out_ready, HT)
                down(b0, 1, None, I1)

                def pair_steps(lo, hi):
                    with pe.Fori(0, (hi - lo) // 2) as turn:
                        q = turn * 2 + lo
                        for j in range(2):
                            s = (1 + j) % 2
                            pe.wait_ge(lo_ready, q + (j + 1)) if h == 0 else None
                            slots_free(q + (b0 + 1 + j))
                            project(q + (b0 + 1 + j), s, q + j, h)
                            down(q + (b0 + j), 1 - s, q + (j - 1))

                if h == 0:
                    pair_steps(1, 15)
                    prep_logits(1)
                    prep_wt(1)
                    pe.wait_ge(wt_copied, 2)
                    pair_steps(15, 31)
                else:
                    pair_steps(1, 31)
                pe.wait_ge(lo_ready, PAIRS)
                slots_free(b0 + 32)
                project(b0 + 32, 1, 31, h)
                down(b0 + 31, 0, 30)
                down(b0 + 32, 1, 31)

        @block.vector
        def _(dve):
            v = nc.vector
            steps = Steps(dve, dve_step)
            asked = [0]

            def moments(src, t):
                return v.bn_stats(bn[:, t, :], src)

            def norm_request(tiles, sources, mul, eps):
                r = asked[0]
                asked[0] += 1
                marks = [steps(moments(src, t)) for t, src in zip(tiles, sources)]
                for t, m in zip(tiles, marks):
                    steps.need(m)
                    m = steps(v.bn_aggr(mv[:, t, :], bn[:, t, :]))
                steps.need(m)
                v.tensor_scalar(var_in[:, r, 0:len(tiles)], mv[:, tiles[0]:tiles[-1] + 1, 1], mul, eps,
                                ALU.mult, ALU.add).then_inc(var_ready, 1)
                return r

            v.memset(ones2[:, :], 1.0).then_inc(ones2_set, 1)
            dve.wait_ge(small_in, SMALL)
            a = steps(v.tensor_scalar(tern[:, :, :], w0_sb[:, :, :], 0.25, None, ALU.is_gt))
            b_ = steps(v.tensor_scalar(w0_sb[:, :, :], w0_sb[:, :, :], -0.25, None, ALU.is_lt))
            steps.need(b_)
            v.tensor_tensor(tern[:, :, :], tern[:, :, :], w0_sb[:, :, :], ALU.subtract).then_inc(tern_set, 1)
            dve.wait_ge(gates_done, 1)
            dve.wait_ge(act_step, 1)
            a = steps(v.tensor_scalar(k_mix[:, 2:3], tg[:, 4:5], -0.5, 0.5, ALU.mult, ALU.add))
            b_ = steps(v.tensor_scalar(k_mix[:, 3:4], tg[:, 4:5], 0.125, 0.125, ALU.mult, ALU.add))
            steps.need(b_)
            steps(v.tensor_tensor(k_mix[:, 0:1], k_mix[:, 2:3], tg[:, 1:2], ALU.mult))
            steps(v.tensor_tensor(k_mix[:, 1:2], k_mix[:, 3:4], tg[:, 1:2], ALU.mult))

            def center(b):
                dve.wait_ge(x_in[b], 16)
                return norm_request([2 * b, 2 * b + 1], [X[:, 2 * b, :], X[:, 2 * b + 1, :]], 1.0, EPS)

            def normalise(r, tiles, ready):
                dve.wait_ge(rstd_ready, r + 1)
                for k, t in enumerate(tiles):
                    v.tensor_scalar(XN[:, t, :], X[:, t, :], mv[:, t, 0:1], rstd[:, r, k:k + 1],
                                    ALU.subtract, ALU.mult).then_inc(ready, 1)

            def sim_stats(b):
                dve.wait_ge(sim_ready, b + 1)
                return norm_request([2 * b, 2 * b + 1], [ps_sim[b % 2][:, 0:256], ps_sim[b % 2][:, 256:512]],
                                    SIM_SCALE * SIM_SCALE, EPS_SIM)

            def sim_norm(b, r):
                dve.wait_ge(rstd_ready, r + 1)
                t0 = 2 * b
                m = steps(v.tensor_scalar(r16[:, t0:t0 + 2], rstd[:, r, 0:2], SIM_SCALE, None, ALU.mult))
                for k in range(2):
                    v.scalar_tensor_tensor(Z[:, t0 + k, :], ps_sim[b % 2][:, k * 256:(k + 1) * 256],
                                           mv[:, t0 + k, 0:1], gamma_sb[:, :], ALU.subtract, ALU.mult
                                           ).then_inc(sim_used, 1)
                steps.need(m)
                marks = []
                for k in range(2):
                    dve.wait_ge(sim_used, t0 + k + 1)
                    marks.append(steps(v.scalar_tensor_tensor(Z[:, t0 + k, :], Z[:, t0 + k, :], r16[:, t0 + k:t0 + k + 1],
                                                              beta_sb[:, :], ALU.mult, ALU.add)))
                for k in range(2):
                    steps.need(marks[k])
                    marks[k] = steps(v.tensor_reduce(rden[:, t0 + k:t0 + k + 1], Z[:, t0 + k, :], AX_X, ALU.max))
                for k in range(2):
                    steps.need(marks[k])
                    v.tensor_scalar(nmax[:, t0 + k:t0 + k + 1], rden[:, t0 + k:t0 + k + 1], -1.0, None,
                                    ALU.mult).then_inc(z_ready, 1)

            def attend(b):
                t0 = 2 * b
                dve.wait_ge(exp_ready, t0 + 2)
                m = steps(v.reciprocal(rden[:, t0:t0 + 2], den[:, t0:t0 + 2]))
                steps.need(m)
                m = steps(v.tensor_scalar(rden[:, t0:t0 + 2], rden[:, t0:t0 + 2], tg[:, 0:1], None, ALU.mult))
                steps.need(m)
                for k in range(2):
                    m = steps(v.scalar_tensor_tensor(X[:, t0 + k, :], Z[:, t0 + k, :], rden[:, t0 + k:t0 + k + 1],
                                                     X[:, t0 + k, :], ALU.mult, ALU.add))
                steps.need(m)
                return norm_request([t0, t0 + 1], [X[:, t0, :], X[:, t0 + 1, :]], 1.0, EPS)

            def split_rows(b, r):
                normalise(r, [2 * b, 2 * b + 1], xn_ready)
                for t in (2 * b, 2 * b + 1):
                    if t >= 4:
                        dve.wait_ge(xg_ready, t - 3)
                    dve.wait_ge(xn_ready, t + 1)
                    m = steps(v.tensor_copy(rows16[:, t % 4, 0, :], XN[:, t, :]))
                    steps.need(m)
                    m = steps(v.tensor_tensor(rows16[:, t % 4, 1, :], XN[:, t, :], rows16[:, t % 4, 0, :], ALU.subtract))
                split_done[b] = m

            split_done = {}

            def route(t):
                s = t % 2
                lgt = lg0[:, s, :]
                dve.wait_ge(logits_ready, t + 1)
                if t >= 2:
                    dve.wait_ge(exp0_ready, t - 1)
                m = steps(v.tensor_copy(lgt, ps_small[s][:, 256:256 + E0]))
                steps.need(m)
                m = steps(v.max(m8[:, s, :], lgt))
                steps.need(m)
                v.tensor_scalar(nm0[:, t:t + 1], m8[:, s, 0:1], -1.0, None, ALU.mult).then_inc(max_ready, 1)
                m = steps(v.max_index(m8i[:, s, :], m8[:, s, :], lgt))
                steps.need(m)
                m = steps(v.tensor_copy(idxf[:, s:s + 1], m8i[:, s, 0:1]))
                steps.need(m)
                m = steps(v.tensor_scalar(oh[:, s, :], iota[:, :], idxf[:, s:s + 1], None, ALU.is_equal))
                steps.need(m)
                m = steps(v.tensor_reduce(grp[:, s, :], oh[:, s, :].rearrange("p (a b) -> p a b", a=GR), AX_X, ALU.add))
                steps.need(m)
                if t >= 2:
                    dve.wait_ge(xg_ready, t - 1)
                steps.need(split_done[t // 2])
                for g in range(GR):
                    last = v.tensor_scalar(diag[:, s, g, :], ident16[:, :], grp[:, s, g:g + 1], None, ALU.mult)
                last.then_inc(diag_ready, 1)
                dve.wait_ge(exp0_ready, t + 1)
                m = steps(v.reciprocal(wtop[:, t:t + 1], den1[:, t:t + 1]))
                steps.need(m)
                m = steps(v.tensor_scalar(ohw[:, s, :], oh[:, s, :], wtop[:, t:t + 1], tg[:, 2:3], ALU.mult, ALU.mult))
                steps.need(m)
                steps(v.tensor_reduce(c_mem[:, t, :], ohw[:, s, :].rearrange("p (a b) -> p b a", a=GR), AX_X, ALU.add))

            dve.wait_ge(const_set, 4)
            rc = [center(0), center(1)]
            normalise(rc[0], [0, 1], p_ready)
            for b in range(2, B):
                rc.append(center(b))
                normalise(rc[b - 1], [2 * b - 2, 2 * b - 1], p_ready)
            normalise(rc[3], [6, 7], p_ready)
            for b in range(B):
                sim_norm(b, sim_stats(b))
                if b >= 1:
                    ra = attend(b - 1)
                    if b < B - 1:
                        split_rows(b - 1, ra)
            route(0)
            route(1)
            split_rows(B - 2, ra)
            ra = attend(B - 1)
            route(2)
            route(3)
            split_rows(B - 1, ra)
            for t in range(4, T):
                route(t)
            for k in range(HT):
                v.memset(Z[:, 2 * k:2 * k + 2, :], 0.0).then_inc(y_free, 1)
            dve.wait_ge(y_free, HT)

            def experts0(h, bp):
                t1 = bp + HT * h
                rounds = -(-TOPK // 8)
                m = steps(v.tensor_copy(work[:, :], SIM[:, t1, :]))
                done = 0
                for k in range(HT):
                    t = HT * h + k
                    dve.wait_ge(y_ready, bp * HT + (h * BP * HT + k + 1))
                    a = steps(v.scalar_tensor_tensor(Z[:, t, :], ps_y[k][:, 0:256], c_mem[:, t, 2 * bp:2 * bp + 1],
                                                     Z[:, t, :], ALU.mult, ALU.add))
                    upto = rounds * (k + 1) // HT
                    for i in range(done, upto):
                        steps.need(m)
                        m = steps(v.max(t8[:, :], work[:, :]))
                        if i < rounds - 1:
                            steps.need(m)
                            m = steps(v.match_replace(work[:, :], t8[:, :], work[:, :], NEG))
                    done = upto
                    steps.need(a)
                    v.scalar_tensor_tensor(Z[:, t, :], ps_y[k][:, 256:512], c_mem[:, t, 2 * bp + 1:2 * bp + 2],
                                           Z[:, t, :], ALU.mult, ALU.add).then_inc(y_free, 1)
                steps.need(m)
                dve.wait_ge(th_ready, t1 + 1)
                row = SIM[:, t1, :]
                v.scalar_tensor_tensor(row, row, t8[:, (TOPK - 1) % 8:(TOPK - 1) % 8 + 1], th1[:, :],
                                       ALU.is_ge, ALU.mult).then_inc(adj_ready, 1)

            def layer1_rows(h):
                tiles = list(range(4 * h, 4 * h + 4))
                dve.wait_ge(y_free, HT + (h + 1) * BP * HT)
                for t in tiles:
                    m = steps(v.tensor_tensor(Z[:, t, :], Z[:, t, :], scale_sb[:, :], ALU.mult))
                for k in range(2):
                    dve.wait_ge(sym_ready, 2 * h + k + 1)
                    t = 4 * h + 2 * k
                    v.tensor_tensor(SIM[:, t:t + 2, :].rearrange("p t n -> p (t n)"),
                                    SIM[:, t:t + 2, :].rearrange("p t n -> p (t n)"),
                                    (bank[0], bank[1])[k][:, :], ALU.add).then_inc(sym_added, 1)
                steps.need(m)
                for t in tiles:
                    m = steps(v.tensor_tensor(X[:, t, :], X[:, t, :], Z[:, t, :], ALU.add))
                steps.need(m)
                r = norm_request(tiles, [X[:, t, :] for t in tiles], 1.0, EPS)
                dve.wait_ge(rstd_ready, r + 1)
                dve.wait_ge(sym_added, 2 * h + 2)
                for k, t in enumerate(tiles):
                    m = steps(v.tensor_scalar(XN[:, t, :], X[:, t, :], mv[:, t, 0:1], rstd[:, r, k:k + 1],
                                              ALU.subtract, ALU.mult))
                steps.need(m)
                for t in tiles:
                    m = steps(v.scalar_tensor_tensor(X[:, t, :], XN[:, t, :], k_mix[:, 0:1], X[:, t, :], ALU.mult, ALU.add))
                steps.need(m)
                for t in tiles:
                    m = steps(v.scalar_tensor_tensor(X[:, t, :], SIM[:, t, :], k_mix[:, 1:2], X[:, t, :], ALU.mult, ALU.add))
                steps.need(m)
                r = norm_request(tiles, [X[:, t, :] for t in tiles], 1.0, EPS)
                normalise(r, tiles, xn3_ready)

            def top8(h):
                tiles = range(4 * h, 4 * h + 4)
                for u in (2 * h, 2 * h + 1):
                    dve.wait_ge(x16hi_ready, u + 1)
                    a, z = (u % 2) * 256, (u % 2 + 1) * 256
                    v.tensor_tensor(x16[:, h, 1, :, a:z], x3_t[:, u % 2, :, :], x16[:, h, 0, :, a:z],
                                    ALU.subtract).then_inc(x16_ready, 1)
                dve.wait_ge(logits1_ready, 4 * h + 4)
                v.tensor_copy(lg[:, :, :], ps_w[:, 0:320].rearrange("p (t n) -> p t n", t=HT)[:, :, 0:E1 + 1]
                              ).then_inc(logits1_copied, 1)
                dve.wait_ge(logits1_copied, h + 1)
                marks = [steps(v.max(top[:, t % HT, :], lg[:, t % HT, 0:E1])) for t in tiles]
                for t, m in zip(tiles, marks):
                    steps.need(m)
                    v.tensor_scalar(nmax[:, t:t + 1], top[:, t % HT, 0:1], -1.0, None, ALU.mult).then_inc(top_ready, 1)
                marks = [steps(v.match_replace(rep[:, t % HT, :], top[:, t % HT, :], lg[:, t % HT, 0:E1], NEG))
                         for t in tiles]
                for i, t in enumerate(tiles):
                    steps.need(marks[i])
                    dve.wait_ge(exp1_ready, t + 1)
                    marks[i] = steps(v.scalar_tensor_tensor(ex1[:, t % HT, :], rep[:, t % HT, :], NEG, ex1[:, t % HT, :],
                                                            ALU.is_equal, ALU.mult, accum_out=den[:, t:t + 1]))
                a, z = 4 * h, 4 * h + 4
                m2 = steps(v.tensor_scalar(sgt[:, a:z], sgt[:, a:z], 0.5, 0.5, ALU.mult, ALU.add))
                steps.need(m2)
                m = steps(v.reciprocal(rden[:, a:z], den[:, a:z]))
                m2 = steps(v.tensor_copy(ws16[:, :, 0], sgt[:, a:z]))
                steps.need(m)
                marks = [steps(v.tensor_scalar(w16[:, t % HT, 0:E1], ex1[:, t % HT, :], rden[:, t:t + 1], None, ALU.mult))
                         for t in tiles]
                steps.need(m2)
                steps(v.tensor_tensor(ws16[:, :, 1], sgt[:, a:z], ws16[:, :, 0], ALU.subtract))
                for i, t in enumerate(tiles):
                    steps.need(marks[i])
                    last = v.scalar_tensor_tensor(w16[:, t % HT, E1:], ex1[:, t % HT, :], rden[:, t:t + 1],
                                                  w16[:, t % HT, 0:E1], ALU.mult, ALU.subtract)
                    last.then_inc(w16_ready, 1)

            for bp in range(BP):
                experts0(0, bp)
            experts0(1, 0)
            layer1_rows(0)
            experts0(1, 1)
            experts0(1, 2)
            top8(0)
            experts0(1, 3)
            layer1_rows(1)

            NS = PAIRS + 1

            def combine(n, s, m=P, first=False):
                dve.wait_ge(up_ready, n + 1)
                dve.wait_ge(silu_ready, n + 1)
                v.tensor_tensor(gated[0:m, s, :], silu[0:m, s, :], ps_up[s][0:m, :], ALU.mult).then_inc(gated_ready, 1)
                dve.wait_ge(wb_ready, n + 1)
                dve.wait_ge(gated_ready, n + 1)
                if not first:
                    dve.wait_ge(ihi_ready, n - 1)
                v.tensor_tensor(inter[0:m, s, :], gated[0:m, s, :], ps_w[0:m, :], ALU.mult).then_inc(inter_ready, 1)
                dve.wait_ge(inter_ready, n + 1)
                dve.wait_ge(ihi_ready, n + 1)
                v.tensor_tensor(inter16[0:m, s, 1, :], inter[0:m, s, :], inter16[0:m, s, 0, :], ALU.subtract
                                ).then_inc(ilo_ready, 1)

            def pair_steps(b0, lo, hi):
                with dve.Fori(0, (hi - lo) // 2) as turn:
                    q = turn * 2 + lo
                    for j in range(2):
                        combine(q + (b0 + 1 + j), (1 + j) % 2)

            for h in range(2):
                b0 = h * NS
                combine(b0, 1, I1, first=(h == 0))
                combine(b0 + 1, 0, first=(h == 0))
                if h == 0:
                    pair_steps(b0, 1, 15)
                    top8(1)
                    pair_steps(b0, 15, 31)
                else:
                    pair_steps(b0, 1, 31)
                combine(b0 + 32, 1)
                dve.wait_ge(down_ready, b0 + NS)
                for k in range(HT):
                    t = HT * h + k
                    v.scalar_tensor_tensor(X[:, t, :], ps_down[k // 2][:, (k % 2) * D:(k % 2 + 1) * D], tg[:, 3:4],
                                           X[:, t, :], ALU.mult, ALU.add).then_inc(out_ready, 1)


def kernel(**inputs):
    import numpy as np
    import concourse.bacc as bacc
    from concourse.bass_utils import run_bass_kernel_spmd

    a = {k: np.asarray(w) for k, w in inputs.items()}
    laid = {
        "x": a["x"],
        "ctx_t": a["ctx_512"].reshape(B * S, DC).T,
        "g_xattn": a["g_xattn"], "g_ffn": a["g_ffn"],
        "wk_t": a["L0_xattn_W_k"].T, "b_k": a["L0_xattn_b_k"],
        "ln_gamma": a["L0_xattn_ln_gamma"], "ln_beta": a["L0_xattn_ln_beta"],
        "w0_t": a["L0_ffn_weight"].T, "scale0": a["L0_ffn_scale"],
        "masks_t": a["L0_ffn_expert_masks"].transpose(2, 0, 1).reshape(D, E0 // 2, 2 * D),
        "router_t": a["L0_ffn_router_w"].T,
        "wq1_t": a["L1_xattn_Wq"].T, "wk1_t": a["L1_xattn_Wk"].T,
        "gamma_raw": a["L1_xattn_gamma_raw"].reshape(1),
        "gate_t": a["L1_ffn_gate_w"].T,
        "gu_t": a["L1_ffn_gu_w"].reshape(PAIRS, 2, 2, I1, D).transpose(4, 0, 2, 1, 3).reshape(D, PAIRS, 4 * I1),
        "dp_t": a["L1_ffn_dp_w"].transpose(0, 2, 1).reshape(E1 * I1, D),
        "shg_t": a["L1_ffn_sh_gate_w"].T, "shu_t": a["L1_ffn_sh_up_w"].T,
        "shd_t": a["L1_ffn_sh_down_w"].T, "shgate_t": a["L1_ffn_sh_gate1_w"].T,
    }
    nc = bacc.Bacc("TRN2", target_bir_lowering=False, num_devices=1)
    arrays, args = {}, []
    for name, w in laid.items():
        w = np.ascontiguousarray(w)
        arrays[f"in_{name}"] = w
        args.append(nc.dram_tensor(f"in_{name}", w.shape, mybir.dt.from_np(w.dtype), kind="ExternalInput").ap())
    out = nc.dram_tensor("out", (B, S, D), F32, kind="ExternalOutput").ap()
    flamingo_block(nc, *args, out)
    r = run_bass_kernel_spmd(nc, [arrays], core_ids=[0])
    return r.results[0]["out"]
```

```python
from contextlib import ExitStack

import concourse.bass as bass
from concourse import mybir

ALU = mybir.AluOpType
ACT = mybir.ActivationFunctionType
F32 = mybir.dt.float32
F16 = mybir.dt.float16
U32 = mybir.dt.uint32
AX_X = mybir.AxisListType.X

P = 128
B, S, D = 4, 256, 256
DC = 64
T = B * S // P
HT = T // 2
HN = HT * P
C = D // P
E0 = 32
GR, MB = 4, 8
BP = MB // 2
E1, I1 = 64, 64
PAIRS = E1 // 2
TOPK = int(S * 0.3)
NEG = -3.0e38
EPS = 1e-5
EPS_SIM = 1e-6
SIM_SCALE = D ** -0.5
SIM1_SCALE = 1.0 / 16.0


class Steps:

    def __init__(self, engine, sem):
        self.engine, self.sem, self.n = engine, sem, 0

    def __call__(self, instruction):
        instruction.then_inc(self.sem, 1)
        self.n += 1
        return self.n

    def need(self, step):
        self.engine.wait_ge(self.sem, step)


def flamingo_block(nc, x, ctx_t, g_xattn, g_ffn, wk_t, b_k, ln_gamma, ln_beta, w0_t, scale0, masks_t,
                   router_t, wq1_t, wk1_t, gamma_raw, gate_t, gu_t, dp_t, shg_t, shu_t, shd_t, shgate_t, out):
    with ExitStack() as stack:
        def sb(name, shape, dt=F32):
            return stack.enter_context(nc.sbuf_tensor(name, shape, dt))

        def sem(name):
            return stack.enter_context(nc.semaphore(name))

        X = sb("X", [P, T, D])
        XN = sb("XN", [P, T, D])
        Z = sb("Z", [P, T, D])
        SIM = sb("SIM", [P, T, S])
        gu16 = sb("gu16", [P, PAIRS, 2, C, 256], F16)
        m16 = gu16[:, PAIRS // 2:, :, :, :].rearrange("p a b c d -> p (a b c d)").rearrange(
            "p (c e o) -> p c e o", c=C, e=E0)
        rows16 = gu16[:, 12:14, :, :, :].rearrange("p a b c d -> p (a b c d)").rearrange(
            "p (k s n) -> p k s n", k=HT, s=2)
        diag = gu16[:, 14:16, :, :, :].rearrange("p a b c d -> p (a b c d)").rearrange(
            "p (k g n) -> p k g n", k=HT, g=GR)
        stage_dp = sb("stage_dp", [P, 2 * C * GR * 2 * D])
        mask_stage = stage_dp[:, :].rearrange("p (s c a n) -> p s c a n", s=2, c=C, a=GR)
        dp16 = stage_dp[:, :].bitcast(F16).rearrange("p (q s n) -> p q s n", q=PAIRS, s=2)
        xg = sb("xg", [P, T, 2, C, GR * P], F16)
        act_area = xg[:, :, :, :, :].rearrange("p a b c d -> p (a b c d)")
        silu = act_area[:, 0:2048].bitcast(F32).rearrange("p (s n) -> p s n", s=2)
        gated = act_area[:, 2048:4096].bitcast(F32).rearrange("p (s n) -> p s n", s=2)
        inter = act_area[:, 4096:6144].bitcast(F32).rearrange("p (s n) -> p s n", s=2)
        inter16 = act_area[:, 6144:8192].rearrange("p (s h n) -> p s h n", s=2, h=2)
        stage = sb("stage", [P, 2, 768])
        early = sb("early", [P, 5120])
        ctx_sb = early[0:DC + 1, 0:1024]
        kv_t = early[0:DC, 1024:2048]
        kv = early[:, 2048:2560].rearrange("p (t d) -> p t d", d=DC)
        q_t = early[0:DC, 2560:3072]
        k_t = early[0:DC, 3072:3584]
        p_t = early[:, 3584:4608].rearrange("p (s c n) -> p s c n", s=2, c=C)
        o_t = early[0:DC, 4608:5120].rearrange("p (s n) -> p s n", s=2)
        late = early[:, :].bitcast(F16)
        x16 = late[:, 0:4096].rearrange("p (h s c n) -> p h s c n", h=2, s=2, c=C)
        pick = late[:, 4096:8192]
        w_t = late[:, 8192:9216].rearrange("p (h n) -> p h n", h=2)
        ws_t = late[0:2, 9216:10240].rearrange("p (h n) -> p h n", h=2)

        xn_t = sb("xn_t", [P, 2, C, 2 * P])
        gamma_sb = sb("gamma_sb", [P, S])
        beta_sb = sb("beta_sb", [P, S])
        scale_sb = sb("scale_sb", [P, D])
        ident = sb("ident", [P, P])
        ident16 = sb("ident16", [P, P], F16)
        iota = sb("iota", [P, E0])
        minus_half = sb("minus_half", [P, 4])
        wk_sb = sb("wk_sb", [DC + 1, DC])
        wq1_sb = sb("wq1_sb", [DC, DC])
        wk1_sb = sb("wk1_sb", [DC, DC])
        tern = sb("tern", [P, C, D])
        w0_sb = Z[:, 6:8, :]
        shared_stage = Z[:, 4, :].rearrange("p (c n) -> p c n", c=C)
        shared_dn_stage = Z[0:I1, 5, :]
        router_sb = sb("router_sb", [P, C, E0])
        gate_sb = sb("gate_sb", [P, C, E1 + 1])
        gates = sb("gates", [P, 5])
        tg = sb("tg", [P, 5])
        k_mix = sb("k_mix", [P, 4])
        shared16 = sb("shared16", [P, 2, C, 128], F16)
        shared_dn16 = sb("shared_dn16", [I1, 2, D], F16)
        bn = sb("bn", [P, T, 6])
        mv = sb("mv", [P, T, 2])
        NR = 10
        var_in = sb("var_in", [P, NR, 4])
        rstd = sb("rstd", [P, NR, 4])
        tiny = sb("tiny", [P, 8, T])
        c_mem = sb("c_mem", [P, T, MB])
        lg0 = sb("lg0", [P, HT, E0])
        oh = sb("oh", [P, HT, E0])
        ohw = sb("ohw", [P, HT, E0])
        grp = sb("grp", [P, HT, GR])
        m8i = sb("m8i", [P, HT, 8], U32)
        idxf = sb("idxf", [P, HT])
        work = sb("work", [P, S])
        t8 = sb("t8", [P, 8])
        lg = sb("lg", [P, HT, E1 + 1])
        rep = Z[:, 0, :].rearrange("p (t n) -> p t n", t=HT)
        ex1 = Z[:, 1, :].rearrange("p (t n) -> p t n", t=HT)
        w16 = Z[:, 2, :].bitcast(F16).rearrange("p (t n) -> p t n", t=HT)
        top = sb("top", [P, HT, 8])
        ws16 = sb("ws16", [P, HT, 2], F16)
        ones2 = sb("ones2", [2, I1], F16)
        nmax, den, rden, r16, nm0, wtop, den1, sgt = (tiny[:, j, :] for j in range(8))

        bank = [stack.enter_context(nc.psum_tensor(f"bank{j}", [P, 512], F32)) for j in range(8)]
        ps_kv = [bank[3], bank[4]]
        ps_kvr = bank[5]
        ps_tr = bank[1]
        ps_small = bank[2]
        ps_sim = [bank[0], bank[7]]
        ps_sim1 = [bank[5], bank[6]]
        ps_y = [bank[3], bank[4], bank[5], bank[6]]
        ps_grp = [bank[3], bank[4], bank[5], bank[6]], [bank[0], bank[7], bank[0], bank[7]]
        ps_sym = [bank[0], bank[1]], [bank[2], bank[2]]
        ps_gate = [bank[3], bank[4]]
        ps_up = [bank[5], bank[6]]
        ps_w = bank[1]
        ps_prep = bank[2]
        ps_down = [bank[0], bank[7]]

        x_in = [sem(f"x_in{b}") for b in range(B)]
        ctx_in, attn_in, small_in = sem("ctx_in"), sem("attn_in"), sem("small_in")
        w0_in, norm_in, qk_in = sem("w0_in"), sem("norm_in"), sem("qk_in")
        gates_in, late_in = sem("gates_in"), sem("late_in")
        mask_in = [sem(f"mask_in{s}") for s in range(2)]
        stage_in = [sem(f"stage_in{s}") for s in range(2)]
        ones_set, const_set, tern_set = sem("ones_set"), sem("const_set"), sem("tern_set")
        pool_step, dve_step, act_step = sem("pool_step"), sem("dve_step"), sem("act_step")
        gates_done = sem("gates_done")
        var_ready, rstd_ready = sem("var_ready"), sem("rstd_ready")
        mask_ready = sem("mask_ready")
        proj_ready, proj_copied = sem("proj_ready"), sem("proj_copied")
        p_ready, pt_ready, pt_copied = sem("p_ready"), sem("pt_ready"), sem("pt_copied")
        o_ready, o_copied, sim_ready = sem("o_ready"), sem("o_copied"), sem("sim_ready")
        sim_used, z_ready, exp_ready = sem("sim_used"), sem("z_ready"), sem("exp_ready")
        sim1_ready, sim1_copied = sem("sim1_ready"), sem("sim1_copied")
        xn_ready, xnt_ready, xnt_copied = sem("xn_ready"), sem("xnt_ready"), sem("xnt_copied")
        logits_ready, max_ready, exp0_ready = sem("logits_ready"), sem("max_ready"), sem("exp0_ready")
        diag_ready, xg_ready, xg_copied = sem("diag_ready"), sem("xg_ready"), sem("xg_copied")
        y_ready, y_free = sem("y_ready"), sem("y_free")
        th_ready, adj_ready, sym_ready = sem("th_ready"), sem("adj_ready"), sem("sym_ready")
        hi_ready, lo_ready = sem("hi_ready"), sem("lo_ready")
        xn3_ready, x3t_ready, x3t_copied = sem("xn3_ready"), sem("x3t_ready"), sem("x3t_copied")
        x16hi_ready, x16_ready = sem("x16hi_ready"), sem("x16_ready")
        logits1_ready, top_ready, exp1_ready = sem("logits1_ready"), sem("top_ready"), sem("exp1_ready")
        w16_ready, wt_ready, wt_copied = sem("w16_ready"), sem("wt_ready"), sem("wt_copied")
        wst_ready, wst_copied = sem("wst_ready"), sem("wst_copied")
        pick_set, shared_hi, shared_set = sem("pick_set"), sem("shared_hi"), sem("shared_set")
        gate_ready, up_ready, wb_ready = sem("gate_ready"), sem("up_ready"), sem("wb_ready")
        silu_ready, gated_ready, inter_ready = sem("silu_ready"), sem("gated_ready"), sem("inter_ready")
        ihi_ready, ilo_ready = sem("ihi_ready"), sem("ilo_ready")
        down_ready = sem("down_ready")
        out_ready, out_done = sem("out_ready"), sem("out_done")
        ones2_set, logits1_copied, sym_added = (
            sem("ones2_set"), sem("logits1_copied"), sem("sym_added"))

        x_d = x.rearrange("b s d -> (b s) d").rearrange("(t p) d -> p t d", p=P)
        out_d = out.rearrange("b s d -> (b s) d").rearrange("(t p) d -> p t d", p=P)
        mask_d = masks_t.rearrange("(c p) (a m) n -> p c a m n", p=P, a=GR)
        gu_d = gu_t.rearrange("(c p) q n -> p c q n", p=P)
        dp_d = dp_t.rearrange("(q p) n -> p q n", p=P)
        stage_gu = [stage[:, s, 0:512].rearrange("p (c n) -> p c n", c=C) for s in range(2)]
        stage_dn = [stage[:, s, 512:768] for s in range(2)]
        GC = C * GR

        block = stack.enter_context(nc.Block())

        @block.sync
        def _(sp):
            def load_row(dst, src, signal):
                sp.dma_start(dst, src.rearrange("(a d) -> a d", a=1).to_broadcast([P, src.shape[0]])
                             ).then_inc(signal, 16)

            for b in range(B):
                sp.dma_start(X[:, 2 * b:2 * b + 2, :], x_d[:, 2 * b:2 * b + 2, :]).then_inc(x_in[b], 16)
            sp.dma_start(w0_sb, w0_t.rearrange("(c p) n -> p c n", p=P)).then_inc(w0_in, 16)
            load_row(gamma_sb[:, :], ln_gamma, norm_in)
            load_row(beta_sb[:, :], ln_beta, norm_in)

            def load_masks(bp):
                if bp >= 2:
                    sp.wait_ge(mask_ready, GC * (bp - 1))
                for c in range(C):
                    sp.dma_start(mask_stage[:, bp % 2, c, :, :],
                                 mask_d[:, c, :, bp, :]).then_inc(mask_in[bp % 2], 16)

            load_masks(0)
            sp.dma_start(wq1_sb[:, :], wq1_t).then_inc(qk_in, 16)
            sp.dma_start(wk1_sb[:, :], wk1_t).then_inc(qk_in, 16)
            load_row(gates[:, 0:2], g_xattn, gates_in)
            load_row(gates[:, 2:4], g_ffn, gates_in)
            load_row(gates[:, 4:5], gamma_raw, gates_in)
            sp.dma_start(router_sb[:, :, :], router_t.rearrange("(c p) n -> p c n", p=P)).then_inc(small_in, 16)
            sp.dma_start(shared_stage[:, :, 0:I1], shg_t.rearrange("(c p) n -> p c n", p=P)).then_inc(small_in, 16)
            sp.dma_start(shared_stage[:, :, I1:128], shu_t.rearrange("(c p) n -> p c n", p=P)).then_inc(small_in, 16)
            sp.dma_start(shared_dn_stage, shd_t).then_inc(small_in, 16)
            load_masks(1)
            sp.dma_start(gate_sb[:, :, 0:E1], gate_t.rearrange("(c p) n -> p c n", p=P)).then_inc(late_in, 16)
            sp.dma_start(gate_sb[:, 0, E1:E1 + 1], shgate_t[0:P, :]).then_inc(late_in, 16)
            sp.dma_start(gate_sb[:, 1, E1:E1 + 1], shgate_t[P:D, :]).then_inc(late_in, 16)
            load_row(scale_sb[:, :], scale0, late_in)
            load_masks(2)
            load_masks(3)

            def load_pair(q, s):
                sp.dma_start(stage_gu[s], gu_d[:, :, bass.ds(q, 1), :].rearrange("p c q n -> p c (q n)")
                             ).then_inc(stage_in[s], 16)
                sp.dma_start(stage_dn[s], dp_d[:, bass.ds(q, 1), :].rearrange("p q n -> p (q n)")
                             ).then_inc(stage_in[s], 16)

            load_pair(0, 0)
            load_pair(1, 1)
            with sp.Fori(0, (PAIRS - 2) // 2) as turn:
                q = turn * 2 + 2
                for s in range(2):
                    sp.wait_ge(lo_ready, q + (s - 1))
                    load_pair(q + s, s)
            for t in range(T):
                sp.wait_ge(out_ready, t + 1)
                sp.dma_start(out_d[:, t, :], X[:, t, :]).then_inc(out_done, 16)
            sp.wait_ge(out_done, 16 * T)

        @block.gpsimd
        def _(pool):
            steps = Steps(pool, pool_step)
            nc.gpsimd.memset(ctx_sb[DC:DC + 1, :], 1.0).then_inc(ones_set, 1)
            pool.wait_ge(ones_set, 1)
            nc.gpsimd.memset(minus_half[:, :], -0.5).then_inc(const_set, 1)
            a = steps(nc.gpsimd.memset(ident[:, :], 0.0))
            b16 = steps(nc.gpsimd.memset(ident16[:, :], 0.0))
            for ready, m in ((a, ident), (b16, ident16)):
                steps.need(ready)
                nc.gpsimd.affine_select(out=m[:, :], in_=m[:, :], compare_op=ALU.not_equal, fill=1.0, base=0,
                                        pattern=[[-1, P]], channel_multiplier=1).then_inc(const_set, 1)
            nc.gpsimd.iota(iota[:, :], pattern=[[1, E0]], base=0, channel_multiplier=0,
                           allow_small_or_imprecise_dtypes=True).then_inc(const_set, 1)
            pool.wait_ge(const_set, 1)

            def rsqrt(r, n):
                pool.wait_ge(var_ready, r + 1)
                nc.gpsimd.tensor_tensor(rstd[:, r, 0:n], var_in[:, r, 0:n], minus_half[:, 0:n],
                                        ALU.pow).then_inc(rstd_ready, 1)

            def mask_piece(n):
                bp, c, g = n // (C * GR), n // GR % C, n % GR
                if n == 0:
                    pool.wait_ge(tern_set, 1)
                if n % (C * GR) == 0:
                    pool.wait_ge(mask_in[bp % 2], 16 * C * (bp // 2 + 1))
                e = g * MB + 2 * bp
                for m in range(2):
                    last = nc.gpsimd.tensor_tensor(m16[:, c, e + m, :], mask_stage[:, bp % 2, c, g, m * D:(m + 1) * D],
                                                   tern[:, c, :], ALU.mult)
                last.then_inc(mask_ready, 1)

            upto = (0, 3, 11, 22, 27, GC * BP)
            done = 0
            for r in range(6):
                rsqrt(r, HT)
                if r == 3:
                    pool.wait_ge(shared_hi, 2)
                    nc.gpsimd.tensor_tensor(shared16[:, 1, :, :], shared_stage, shared16[:, 0, :, :],
                                            ALU.subtract).then_inc(shared_set, 1)
                    nc.gpsimd.tensor_tensor(shared_dn16[:, 1, :], shared_dn_stage, shared_dn16[:, 0, :],
                                            ALU.subtract).then_inc(shared_set, 1)
                for n in range(done, upto[r]):
                    mask_piece(n)
                done = upto[r]
            pool.wait_ge(sim1_ready, 2 * 2)
            pool.wait_ge(sim_ready, B)
            a = steps(nc.gpsimd.memset(pick, 0.0))
            pick3 = pick.rearrange("p (e j) -> p e j", e=E1)
            steps.need(a)
            for base in (0, -E1):
                nc.gpsimd.affine_select(out=pick3, in_=pick3, compare_op=ALU.not_equal, fill=1.0, base=base,
                                        pattern=[[-1, E1], [0, I1]], channel_multiplier=1).then_inc(pick_set, 1)
                pool.wait_ge(pick_set, 1)

            def low_half(q, s):
                pool.wait_ge(hi_ready, q + 1)
                nc.gpsimd.tensor_tensor(gu16[:, bass.ds(q, 1), 1, :, :].rearrange("p q c n -> p (q c) n"),
                                        stage_gu[s], gu16[:, bass.ds(q, 1), 0, :, :].rearrange("p q c n -> p (q c) n"),
                                        ALU.subtract)
                nc.gpsimd.tensor_tensor(dp16[:, bass.ds(q, 1), 1, :].rearrange("p q n -> p (q n)"), stage_dn[s],
                                        dp16[:, bass.ds(q, 1), 0, :].rearrange("p q n -> p (q n)"),
                                        ALU.subtract).then_inc(lo_ready, 1)

            with pool.Fori(0, (PAIRS // 2 - 0) // 2) as turn:
                q = turn * 2 + 0
                for s in range(2):
                    low_half(q + s, s)
            rsqrt(6, HT)
            rsqrt(7, HT)
            with pool.Fori(0, (PAIRS - PAIRS // 2) // 2) as turn:
                q = turn * 2 + PAIRS // 2
                for s in range(2):
                    low_half(q + s, s)
            rsqrt(8, HT)
            rsqrt(9, HT)

        @block.scalar
        def _(act):
            def copy(dst, src, scale=1.0):
                return nc.scalar.activation(dst, src, ACT.Copy, scale=scale)

            act.dma_start(ctx_sb[0:DC, :], ctx_t).then_inc(ctx_in, 16)
            act.dma_start(wk_sb[0:DC, :], wk_t).then_inc(attn_in, 16)
            act.dma_start(wk_sb[DC:DC + 1, :], b_k.rearrange("(a d) -> a d", a=1)).then_inc(attn_in, 16)

            for h in range(2):
                act.wait_ge(proj_ready, h + 1)
                copy(kv_t[:, h * 512:(h + 1) * 512], ps_kv[h][0:DC, :]).then_inc(proj_copied, 1)
            act.wait_ge(proj_ready, 3)
            copy(kv[:, :, :].rearrange("p t d -> p (t d)"), ps_kvr[:, :]).then_inc(proj_copied, 1)

            def attention_rows(b):
                act.wait_ge(pt_ready, b + 1)
                if b >= 2:
                    act.wait_ge(o_ready, b - 1)
                copy(p_t[:, b % 2, :, :].rearrange("p c n -> p (c n)"), ps_tr[:, :]).then_inc(pt_copied, 1)
                act.wait_ge(o_ready, b + 1)
                if b >= 2:
                    act.wait_ge(sim_ready, b - 1)
                copy(o_t[:, b % 2, :], ps_small[0:DC, 0:256]).then_inc(o_copied, 1)

            def softmax_rows(h):
                for t in range(HT * h, HT * h + HT):
                    act.wait_ge(z_ready, h + 1)
                    nc.scalar.activation(Z[:, t, :], Z[:, t, :], ACT.Exp, bias=nmax[:, t:t + 1],
                                         accum_out=den[:, t:t + 1]).then_inc(exp_ready, 1)

            attention_rows(0)
            attention_rows(1)
            for h in range(2):
                for j, dst in enumerate((q_t, k_t)):
                    act.wait_ge(proj_ready, 4 + 2 * h + j)
                    copy(dst, ps_kv[j][0:DC, :]).then_inc(proj_copied, 1)
                for k in range(2):
                    act.wait_ge(sim1_ready, 2 * h + k + 1)
                    t = 4 * h + 2 * k
                    copy(SIM[:, t:t + 2, :].rearrange("p t n -> p (t n)"), ps_sim1[k][:, :],
                         SIM1_SCALE).then_inc(sim1_copied, 1)
            act.wait_ge(gates_in, 16 * 3)
            nc.scalar.activation(tg[:, 0:4], gates[:, 0:4], ACT.Tanh).then_inc(act_step, 1)
            nc.scalar.activation(tg[:, 4:5], gates[:, 4:5], ACT.Tanh, scale=0.5).then_inc(gates_done, 1)
            softmax_rows(0)
            act.wait_ge(small_in, 16 * 4)
            copy(shared16[:, 0, :, :], shared_stage).then_inc(shared_hi, 1)
            copy(shared_dn16[:, 0, :], shared_dn_stage).then_inc(shared_hi, 1)
            attention_rows(2)
            attention_rows(3)

            def route0(h):
                for u in (2 * h, 2 * h + 1):
                    act.wait_ge(xnt_ready, u + 1)
                    if u >= 2:
                        act.wait_ge(logits_ready, h)
                    copy(xn_t[:, u % 2, :, :].rearrange("p c n -> p (c n)"), ps_tr[:, :]).then_inc(xnt_copied, 1)
                act.wait_ge(max_ready, h + 1)
                for t in range(HT * h, HT * h + HT):
                    last = nc.scalar.activation(ohw[:, t % HT, :], lg0[:, t % HT, :], ACT.Exp, bias=nm0[:, t:t + 1],
                                                accum_out=den1[:, t:t + 1])
                last.then_inc(exp0_ready, 1)

            def grouped(t):
                for n in range(2 * C):
                    act.wait_ge(xg_ready, 2 * C * t + n + 1)
                    copy(xg[:, t, n // C, n % C, :], ps_grp[t // HT][n][:, :]).then_inc(xg_copied, 1)

            def tanh_rows(h):
                rows = XN[:, HT * h:HT * h + HT, :].rearrange("p t n -> p (t n)")
                nc.scalar.activation(rows, SIM[:, HT * h:HT * h + HT, :].rearrange("p t n -> p (t n)"), ACT.Tanh,
                                     scale=0.5).then_inc(act_step, 1)
                act.wait_ge(act_step, h + 2)
                nc.scalar.activation(rows, rows, ACT.Copy, bias=1.0).then_inc(th_ready, 1)

            def high_half(q, s, turn):
                act.wait_ge(stage_in[s], turn)
                copy(gu16[:, bass.ds(q, 1), 0, :, :].rearrange("p q c n -> p (q c) n"), stage_gu[s])
                copy(dp16[:, bass.ds(q, 1), 0, :].rearrange("p q n -> p (q n)"), stage_dn[s]).then_inc(hi_ready, 1)

            def high_halves(lo, hi):
                with act.Fori(0, (hi - lo) // 2) as turn:
                    for s in range(2):
                        high_half(turn * 2 + (lo + s), s, turn * 32 + (lo * 16 + 32))

            route0(0)
            for t in range(HT):
                grouped(t)
            tanh_rows(0)
            softmax_rows(1)
            act.wait_ge(mask_ready, GC * BP)
            high_halves(0, 4)
            route0(1)
            high_halves(4, 8)
            for t in range(HT, T):
                grouped(t)
            tanh_rows(1)
            high_halves(8, 16)

            def prep_rows(h):
                for u in (2 * h, 2 * h + 1):
                    act.wait_ge(x3t_ready, u + 1)
                    if u >= 2:
                        act.wait_ge(x16_ready, u - 1)
                        act.wait_ge(logits1_ready, h)
                    copy(xn_t[:, u % 2, :, :].rearrange("p c n -> p (c n)"), ps_prep[:, :]).then_inc(x3t_copied, 1)
                    act.wait_ge(x3t_copied, u + 1)
                    copy(x16[:, h, 0, :, (u % 2) * 256:(u % 2 + 1) * 256], xn_t[:, u % 2, :, :]).then_inc(x16hi_ready, 1)

            def top_rows(h):
                for t in range(4 * h, 4 * h + 4):
                    act.wait_ge(top_ready, h + 1)
                    nc.scalar.activation(ex1[:, t % HT, :], lg[:, t % HT, 0:E1], ACT.Exp, bias=nmax[:, t:t + 1])
                    nc.scalar.activation(sgt[:, t:t + 1], lg[:, t % HT, E1:E1 + 1], ACT.Tanh,
                                         scale=0.5).then_inc(exp1_ready, 1)

            def prep_weights(h):
                act.wait_ge(wt_ready, h + 1)
                copy(w_t[:, h, :], ps_prep[:, :]).then_inc(wt_copied, 1)

            def prep_shared_weight(h):
                act.wait_ge(wst_ready, h + 1)
                copy(ws_t[:, h, :], ps_prep[0:2, :]).then_inc(wst_copied, 1)

            prep_rows(0)
            top_rows(0)
            prep_weights(0)
            prep_shared_weight(0)
            NS = PAIRS + 1

            def silu_step(n, s, m=P):
                act.wait_ge(gate_ready, n + 1)
                act.wait_ge(gated_ready, n - 1)
                nc.scalar.activation(silu[0:m, s, :], ps_gate[s][0:m, :], ACT.Silu).then_inc(silu_ready, 1)

            def high_step(n, s, m=P):
                act.wait_ge(inter_ready, n + 1)
                act.wait_ge(down_ready, n - 1)
                copy(inter16[0:m, s, 0, :], inter[0:m, s, :]).then_inc(ihi_ready, 1)

            for h in range(2):
                b0 = h * NS
                for n in (0, 1):
                    s = (n + 1) % 2
                    act.wait_ge(gate_ready, b0 + n + 1)
                    if b0 + n >= 2:
                        act.wait_ge(gated_ready, b0 + n - 1)
                    m = I1 if n == 0 else P
                    nc.scalar.activation(silu[0:m, s, :], ps_gate[s][0:m, :], ACT.Silu).then_inc(silu_ready, 1)
                    act.wait_ge(inter_ready, b0 + n + 1)
                    if b0 + n >= 2:
                        act.wait_ge(down_ready, b0 + n - 1)
                    copy(inter16[0:m, s, 0, :], inter[0:m, s, :]).then_inc(ihi_ready, 1)

                def pair_steps(lo, hi, convert=False):
                    def two(q, turn):
                        for j in range(2):
                            silu_step(q + (b0 + 1 + j), (1 + j) % 2)
                            high_step(q + (b0 + 1 + j), (1 + j) % 2)
                            if convert:
                                high_half(q + (PAIRS // 2 - 1 + j), j, q * 16 + (16 * (PAIRS // 2 - 1) + 32))
                    if hi - lo == 2:
                        two(lo, None)
                    else:
                        with act.Fori(0, (hi - lo) // 2) as turn:
                            two(turn * 2 + lo, turn)

                if h == 0:
                    pair_steps(1, 17, convert=True)
                    pair_steps(17, 27)
                    prep_rows(1)
                    pair_steps(27, 29)
                    top_rows(1)
                    pair_steps(29, 31)
                    prep_weights(1)
                else:
                    pair_steps(1, 31)
                silu_step(b0 + 32, 1)
                high_step(b0 + 32, 1)
                if h == 0:
                    prep_shared_weight(1)

        @block.tensor
        def _(pe):
            mm = nc.tensor.matmul

            pe.wait_ge(ones_set, 1)
            pe.wait_ge(ctx_in, 16)
            pe.wait_ge(attn_in, 32)
            for h in range(2):
                mm(ps_kv[h][0:DC, :], wk_sb[:, :], ctx_sb[:, h * 512:(h + 1) * 512], start=True, stop=True
                   ).then_inc(proj_ready, 1)
            for t in range(T):
                last = mm(ps_kvr[:, t * DC:(t + 1) * DC], ctx_sb[:, t * P:(t + 1) * P], wk_sb[:, :],
                          start=True, stop=True)
            last.then_inc(proj_ready, 1)
            pe.wait_ge(const_set, 4)

            def transpose_p(b):
                pe.wait_ge(p_ready, 2 * b + 2)
                if b >= 1:
                    pe.wait_ge(pt_copied, b)
                for c in range(C):
                    for k in range(2):
                        last = nc.tensor.transpose(ps_tr[:, c * 256 + k * P:c * 256 + (k + 1) * P],
                                                   XN[:, 2 * b + k, c * P:(c + 1) * P], ident[:, :])
                last.then_inc(pt_ready, 1)

            def out_and_sim(b):
                pe.wait_ge(pt_copied, b + 1)
                pe.wait_ge(proj_copied, 3)
                if b >= 1:
                    pe.wait_ge(o_copied, b)
                for c in range(C):
                    last = mm(ps_small[0:DC, 0:256], kv[:, 2 * b + c, :], p_t[:, b % 2, c, :],
                              start=(c == 0), stop=(c == C - 1))
                last.then_inc(o_ready, 1)
                if b == 0:
                    transpose_p(1)
                if b == 2:
                    transpose_p(3)
                pe.wait_ge(o_copied, b + 1)
                if b >= 2:
                    pe.wait_ge(sim_used, 2 * (b - 1))
                for k in range(2):
                    last = mm(ps_sim[b % 2][:, k * 256:(k + 1) * 256], o_t[:, b % 2, k * P:(k + 1) * P],
                              kv_t[:, b * S:(b + 1) * S], start=True, stop=True)
                last.then_inc(sim_ready, 1)

            transpose_p(0)
            out_and_sim(0)
            out_and_sim(1)

            pe.wait_ge(qk_in, 32)
            for h in range(2):
                for j, w in enumerate((wq1_sb, wk1_sb)):
                    if h == 1:
                        pe.wait_ge(proj_copied, 5)
                    mm(ps_kv[j][0:DC, :], w[:, :], ctx_sb[0:DC, h * 512:(h + 1) * 512], start=True, stop=True
                       ).then_inc(proj_ready, 1)
                pe.wait_ge(proj_copied, 5 + 2 * h)
                for k in range(2):
                    if h == 1:
                        pe.wait_ge(sim1_copied, k + 1)
                    for i in range(2):
                        last = mm(ps_sim1[k][:, i * 256:(i + 1) * 256], q_t[:, k * S + i * P:k * S + (i + 1) * P],
                                  k_t[:, k * S:(k + 1) * S], start=True, stop=True)
                    last.then_inc(sim1_ready, 1)

            transpose_p(2)
            out_and_sim(2)
            out_and_sim(3)

            def router(h):
                for u in (2 * h, 2 * h + 1):
                    pe.wait_ge(xn_ready, 2 * u + 2)
                    if u == 0:
                        pe.wait_ge(pt_copied, B)
                    else:
                        pe.wait_ge(xnt_copied, u)
                    for c in range(C):
                        for k in range(2):
                            last = nc.tensor.transpose(ps_tr[:, c * 256 + k * P:c * 256 + (k + 1) * P],
                                                       XN[:, 2 * u + k, c * P:(c + 1) * P], ident[:, :])
                    last.then_inc(xnt_ready, 1)
                pe.wait_ge(xnt_copied, 2 * h + 2)
                if h == 0:
                    pe.wait_ge(o_copied, B)
                else:
                    pe.wait_ge(max_ready, 1)
                for k in range(HT):
                    for c in range(C):
                        last = mm(ps_small[:, k * E0:(k + 1) * E0], xn_t[:, k // 2, c, (k % 2) * P:(k % 2 + 1) * P],
                                  router_sb[:, c, :], start=(c == 0), stop=(c == C - 1))
                last.then_inc(logits_ready, 1)

            def group_rows(t):
                pe.wait_ge(diag_ready, t + 1)
                for n in range(2 * C):
                    if t == 0:
                        pe.wait_ge(sim1_copied, B)
                        pe.wait_ge(proj_copied, 7)
                    elif t < HT:
                        pe.wait_ge(xg_copied, 2 * C * (t - 1) + n + 1)
                    elif t == HT and n < 2:
                        pe.wait_ge(sim_used, T)
                    else:
                        pe.wait_ge(xg_copied, 2 * C * t + n - 1)
                    mm(ps_grp[t // HT][n][:, :], rows16[:, t % 4, n // C, (n % C) * P:(n % C + 1) * P],
                       diag[:, t % HT, :, :].rearrange("p a n -> p (a n)"), start=True, stop=True
                       ).then_inc(xg_ready, 1)

            pe.wait_ge(small_in, 16 * 4)
            router(0)
            for t in range(HT):
                group_rows(t)

            def experts0(h, bp):
                pe.wait_ge(mask_ready, bp * (C * GR) + C * GR if h == 0 else C * GR * BP)
                for k in range(HT):
                    pe.wait_ge(y_free, bp * HT + (h * BP * HT + k + 1))
                    n = 0
                    for s in range(2):
                        for c in range(C):
                            for g in range(GR):
                                last = mm(ps_y[k][:, :], xg[:, HT * h + k, s, c, g * P:(g + 1) * P],
                                          m16[:, c, bass.ds(bp * 2 + g * MB, 2), :].rearrange("p e o -> p (e o)"),
                                          start=(n == 0), stop=(n == 2 * C * GR - 1))
                                n += 1
                    last.then_inc(y_ready, 1)

            def symmetric(h, which=None):
                for k in (0, 1) if which is None else (which,):
                    pe.wait_ge(adj_ready, 4 * h + 2 * k + 2)
                    dst = ps_sym[h][k]
                    if h == 1:
                        pe.wait_ge(wst_copied, 1)
                        pe.wait_ge(sym_added, 2 + k)
                    for i in range(2):
                        for j in range(2):
                            last = nc.tensor.transpose(dst[:, i * 256 + j * P:i * 256 + (j + 1) * P],
                                                       SIM[:, 4 * h + 2 * k + j, i * P:(i + 1) * P], ident[:, :])
                    last.then_inc(sym_ready, 1)

            def prep_logits(h):
                for u in (2 * h, 2 * h + 1):
                    pe.wait_ge(xn3_ready, 2 * u + 2)
                    if u == 2:
                        pe.wait_ge(sym_added, 4)
                    if u >= 1:
                        pe.wait_ge(x3t_copied, u)
                    for c in range(C):
                        for k in range(2):
                            last = nc.tensor.transpose(ps_prep[:, c * 256 + k * P:c * 256 + (k + 1) * P],
                                                       XN[:, 2 * u + k, c * P:(c + 1) * P], ident[:, :])
                    last.then_inc(x3t_ready, 1)
                pe.wait_ge(x3t_copied, 2 * h + 2)
                pe.wait_ge(late_in, 16 * 4)
                for k in range(HT):
                    for c in range(C):
                        last = mm(ps_prep[:, k * 80:k * 80 + E1 + 1], xn_t[:, k // 2, c, (k % 2) * P:(k % 2 + 1) * P],
                                  gate_sb[:, c, :], start=(c == 0), stop=(c == C - 1))
                last.then_inc(logits1_ready, 1)

            def prep_wt(h):
                pe.wait_ge(w16_ready, HT * h + HT)
                for k in range(HT):
                    last = mm(ps_prep[:, k * P:(k + 1) * P], w16[:, k, :], ident16[:, :], start=True, stop=True)
                last.then_inc(wt_ready, 1)

            def prep_wst(h):
                pe.wait_ge(wt_copied, h + 1)
                for k in range(HT):
                    last = mm(ps_prep[0:2, k * P:(k + 1) * P], ws16[:, k, :], ident16[:, :], start=True, stop=True)
                last.then_inc(wst_ready, 1)

            pe.wait_ge(xg_copied, 2 * C * HT)
            with pe.Fori(0, 2) as bp:
                experts0(0, bp)
            router(1)
            experts0(0, 2)
            for t in range(HT, T):
                group_rows(t)
            experts0(0, 3)
            pe.wait_ge(xg_copied, 2 * C * T)
            with pe.Fori(0, 2) as bp:
                experts0(1, bp)
            symmetric(0)
            experts0(1, 2)
            prep_logits(0)
            experts0(1, 3)
            prep_wt(0)
            prep_wst(0)

            NS = PAIRS + 1
            SPLIT = ((0, 0), (0, 1), (1, 0))

            def project(n, s, q, h, m=P):
                for part, (dst, ready) in enumerate(((ps_gate[s], gate_ready), (ps_up[s], up_ready))):
                    k = 0
                    for a, b in SPLIT:
                        for c in range(C):
                            if q is None:
                                w = shared16[:, a, c, part * I1:(part + 1) * I1]
                            else:
                                w = gu16[:, bass.ds(q, 1), a, c, part * P:(part + 1) * P].rearrange("p q n -> p (q n)")
                            last = mm(dst[0:m, :], w, x16[:, h, b, c, :], start=(k == 0), stop=(k == 3 * C - 1))
                            k += 1
                    last.then_inc(ready, 1)
                    if part == 0:
                        if not (isinstance(n, int) and n == 0):
                            pe.wait_ge(inter_ready, n)
                        if q is None:
                            mm(ps_w[0:m, :], ones2[:, :], ws_t[:, h, :], start=True, stop=True).then_inc(wb_ready, 1)
                        else:
                            mm(ps_w[:, :], pick[:, bass.ds(q * P, P)], w_t[:, h, :], start=True, stop=True
                               ).then_inc(wb_ready, 1)

            def down(n, s, q, m=P):
                pe.wait_ge(ilo_ready, n + 1)
                for k in range(HT):
                    dst = ps_down[k // 2][:, (k % 2) * D:(k % 2 + 1) * D]
                    for j, (a, b) in enumerate(SPLIT):
                        if q is None:
                            w = shared_dn16[:, b, :]
                        else:
                            w = dp16[:, bass.ds(q, 1), b, :].rearrange("p q n -> p (q n)")
                        last = mm(dst, inter16[0:m, s, a, k * P:(k + 1) * P], w,
                                  start=(q is None and j == 0 and k % 2 == 0), stop=True, skip_group_check=True)
                last.then_inc(down_ready, 1)

            def slots_free(n):
                pe.wait_ge(silu_ready, n - 1)
                pe.wait_ge(gated_ready, n - 1)

            pe.wait_ge(pick_set, 2)
            pe.wait_ge(ones2_set, 1)
            pe.wait_ge(shared_set, 2)
            for h in range(2):
                b0 = h * NS
                pe.wait_ge(wst_copied, h + 1)
                pe.wait_ge(x16_ready, 2 * h + 2)
                if h == 0:
                    pe.wait_ge(y_free, HT + 2 * BP * HT)
                else:
                    slots_free(b0)
                project(b0, 1, None, h, I1)
                if h == 1:
                    slots_free(b0 + 1)
                pe.wait_ge(lo_ready, 1)
                project(b0 + 1, 0, 0, h)
                if h == 1:
                    pe.wait_ge(out_ready, HT)
                down(b0, 1, None, I1)

                def pair_steps(lo, hi):
                    def two(q):
                        for j in range(2):
                            s = (1 + j) % 2
                            if h == 0:
                                pe.wait_ge(lo_ready, q + (j + 1))
                            slots_free(q + (b0 + 1 + j))
                            project(q + (b0 + 1 + j), s, q + j, h)
                            down(q + (b0 + j), 1 - s, q + (j - 1))
                    if hi - lo == 2:
                        two(lo)
                    else:
                        with pe.Fori(0, (hi - lo) // 2) as turn:
                            two(turn * 2 + lo)

                if h == 0:
                    pair_steps(1, 17)
                    symmetric(1, 0)
                    pair_steps(17, 19)
                    symmetric(1, 1)
                    pair_steps(19, 27)
                    prep_logits(1)
                    pair_steps(27, 31)
                    prep_wt(1)
                else:
                    pair_steps(1, 31)
                pe.wait_ge(lo_ready, PAIRS)
                slots_free(b0 + 32)
                project(b0 + 32, 1, 31, h)
                down(b0 + 31, 0, 30)
                if h == 0:
                    prep_wst(1)
                down(b0 + 32, 1, 31)

        @block.vector
        def _(dve):
            v = nc.vector
            steps = Steps(dve, dve_step)
            asked = [0]

            def moments(src, t):
                return v.bn_stats(bn[:, t, :], src)

            def norm_request(tiles, sources, mul, eps):
                r = asked[0]
                asked[0] += 1
                marks = [steps(moments(src, t)) for t, src in zip(tiles, sources)]
                for t, m in zip(tiles, marks):
                    steps.need(m)
                    m = steps(v.bn_aggr(mv[:, t, :], bn[:, t, :]))
                steps.need(m)
                v.tensor_scalar(var_in[:, r, 0:len(tiles)], mv[:, tiles[0]:tiles[-1] + 1, 1], mul, eps,
                                ALU.mult, ALU.add).then_inc(var_ready, 1)
                return r

            v.memset(ones2[:, :], 1.0).then_inc(ones2_set, 1)

            def tiles_of(h):
                return list(range(HT * h, HT * h + HT))

            def center(h):
                tiles = tiles_of(h)
                for b in (2 * h, 2 * h + 1):
                    dve.wait_ge(x_in[b], 16)
                return norm_request(tiles, [X[:, t, :] for t in tiles], 1.0, EPS)

            def normalise(r, h, ready):
                dve.wait_ge(rstd_ready, r + 1)
                for k, t in enumerate(tiles_of(h)):
                    v.tensor_scalar(XN[:, t, :], X[:, t, :], mv[:, t, 0:1], rstd[:, r, k:k + 1],
                                    ALU.subtract, ALU.mult).then_inc(ready, 1)

            def sim_bank(t):
                return ps_sim[t // 2 % 2][:, (t % 2) * 256:(t % 2 + 1) * 256]

            def similarity(h):
                tiles = tiles_of(h)
                dve.wait_ge(sim_ready, 2 * h + 2)
                r = norm_request(tiles, [sim_bank(t) for t in tiles], SIM_SCALE * SIM_SCALE, EPS_SIM)
                dve.wait_ge(rstd_ready, r + 1)
                a, z = tiles[0], tiles[-1] + 1
                m = steps(v.tensor_scalar(r16[:, a:z], rstd[:, r, :], SIM_SCALE, None, ALU.mult))
                if h == 1:
                    dve.wait_ge(shared_set, 2)
                for t in tiles:
                    v.scalar_tensor_tensor(Z[:, t, :], sim_bank(t), mv[:, t, 0:1], gamma_sb[:, :],
                                           ALU.subtract, ALU.mult).then_inc(sim_used, 1)
                steps.need(m)
                marks = []
                for t in tiles:
                    dve.wait_ge(sim_used, t + 1)
                    marks.append(steps(v.scalar_tensor_tensor(Z[:, t, :], Z[:, t, :], r16[:, t:t + 1], beta_sb[:, :],
                                                              ALU.mult, ALU.add)))
                for i, t in enumerate(tiles):
                    steps.need(marks[i])
                    m = steps(v.tensor_reduce(rden[:, t:t + 1], Z[:, t, :], AX_X, ALU.max))
                steps.need(m)
                v.tensor_scalar(nmax[:, a:z], rden[:, a:z], -1.0, None, ALU.mult).then_inc(z_ready, 1)

            def attend(h):
                tiles = tiles_of(h)
                a, z = tiles[0], tiles[-1] + 1
                dve.wait_ge(exp_ready, z)
                m = steps(v.reciprocal(rden[:, a:z], den[:, a:z]))
                steps.need(m)
                m = steps(v.tensor_scalar(rden[:, a:z], rden[:, a:z], tg[:, 0:1], None, ALU.mult))
                steps.need(m)
                for t in tiles:
                    m = steps(v.scalar_tensor_tensor(X[:, t, :], Z[:, t, :], rden[:, t:t + 1], X[:, t, :],
                                                     ALU.mult, ALU.add))
                steps.need(m)
                r = norm_request(tiles, [X[:, t, :] for t in tiles], 1.0, EPS)
                normalise(r, h, xn_ready)
                marks = []
                for t in tiles:
                    if h == 1:
                        dve.wait_ge(xg_ready, 2 * C * (t - 3))
                    dve.wait_ge(xn_ready, t + 1)
                    marks.append(steps(v.tensor_copy(rows16[:, t % 4, 0, :], XN[:, t, :])))
                for i, t in enumerate(tiles):
                    steps.need(marks[i])
                    m = steps(v.tensor_tensor(rows16[:, t % 4, 1, :], XN[:, t, :], rows16[:, t % 4, 0, :], ALU.subtract))
                return m

            def route(h, split_done):
                tiles = tiles_of(h)
                a, z = tiles[0], tiles[-1] + 1
                dve.wait_ge(logits_ready, h + 1)
                m = steps(v.tensor_copy(lg0[:, :, :], ps_small[:, 0:HT * E0].rearrange("p (t n) -> p t n", t=HT)))
                steps.need(m)
                for k in range(HT):
                    m = steps(v.max(top[:, k, :], lg0[:, k, :]))
                steps.need(m)
                v.tensor_scalar(nm0[:, a:z], top[:, :, 0], -1.0, None, ALU.mult).then_inc(max_ready, 1)
                for k in range(HT):
                    m = steps(v.max_index(m8i[:, k, :], top[:, k, :], lg0[:, k, :]))
                steps.need(m)
                m = steps(v.tensor_copy(idxf[:, :], m8i[:, :, 0]))
                steps.need(m)
                m = steps(v.tensor_tensor(oh[:, :, :], iota[:, None, :].to_broadcast([P, HT, E0]),
                                          idxf[:, :, None].to_broadcast([P, HT, E0]), ALU.is_equal))
                steps.need(m)
                m = steps(v.tensor_reduce(grp[:, :, :], oh[:, :, :].rearrange("p t (a b) -> p t a b", a=GR), AX_X, ALU.add))
                steps.need(m)
                steps.need(split_done)
                for t in tiles:
                    if t >= HT:
                        dve.wait_ge(xg_ready, 2 * C * (t - HT + 1))
                    for g in range(GR):
                        last = v.tensor_scalar(diag[:, t % HT, g, :], ident16[:, :], grp[:, t % HT, g:g + 1], None, ALU.mult)
                    last.then_inc(diag_ready, 1)
                dve.wait_ge(exp0_ready, h + 1)
                m = steps(v.reciprocal(wtop[:, a:z], den1[:, a:z]))
                steps.need(m)
                m = steps(v.tensor_scalar(wtop[:, a:z], wtop[:, a:z], tg[:, 2:3], None, ALU.mult))
                steps.need(m)
                m = steps(v.tensor_tensor(ohw[:, :, :], oh[:, :, :], wtop[:, a:z, None].to_broadcast([P, HT, E0]), ALU.mult))
                steps.need(m)
                steps(v.tensor_reduce(c_mem[:, a:z, :], ohw[:, :, :].rearrange("p t (a b) -> p t b a", a=GR), AX_X, ALU.add))

            ROUNDS = -(-TOPK // 8)
            FIND = 2 * ROUNDS
            found = [0]

            def find_top(t, lo, hi):
                for i in range(lo, hi):
                    if found[0]:
                        steps.need(found[0])
                    if i == 0:
                        found[0] = steps(v.tensor_copy(work[:, :], SIM[:, t, :]))
                    elif i % 2:
                        found[0] = steps(v.max(t8[:, :], work[:, :]))
                    else:
                        found[0] = steps(v.match_replace(work[:, :], t8[:, :], work[:, :], NEG))

            def adjacency(t):
                steps.need(found[0])
                dve.wait_ge(th_ready, t // HT + 1)
                k = (TOPK - 1) % 8
                v.scalar_tensor_tensor(SIM[:, t, :], SIM[:, t, :], t8[:, k:k + 1], XN[:, t, :], ALU.is_ge, ALU.mult
                                       ).then_inc(adj_ready, 1)

            def experts0(h, bp, find=None):
                FIND_AT = FIND // HT
                for k in range(HT):
                    t = HT * h + k
                    sums = Z[:, t, :]
                    dve.wait_ge(y_ready, (h * BP + bp) * HT + k + 1)
                    m = steps(v.scalar_tensor_tensor(sums, ps_y[k][:, 0:D], c_mem[:, t, 2 * bp:2 * bp + 1], sums,
                                                     ALU.mult, ALU.add))
                    if find is not None:
                        find_top(find, k * FIND_AT, k * FIND_AT + 1)
                    steps.need(m)
                    v.scalar_tensor_tensor(sums, ps_y[k][:, D:2 * D], c_mem[:, t, 2 * bp + 1:2 * bp + 2], sums,
                                           ALU.mult, ALU.add).then_inc(y_free, 1)
                    if find is not None:
                        find_top(find, k * FIND_AT + 1, (k + 1) * FIND_AT)
                if find is not None:
                    adjacency(find)

            rows_mark = [0, 0]

            def rows_sym(h, k):
                dve.wait_ge(sym_ready, 2 * h + k + 1)
                t = HT * h + 2 * k
                v.tensor_tensor(SIM[:, t:t + 2, :].rearrange("p t n -> p (t n)"),
                                SIM[:, t:t + 2, :].rearrange("p t n -> p (t n)"),
                                ps_sym[h][k][:, :], ALU.add).then_inc(sym_added, 1)

            def rows_scale(h):
                dve.wait_ge(y_free, HT + (h + 1) * BP * HT)
                dve.wait_ge(late_in, 16 * 4)
                for t in tiles_of(h):
                    rows_mark[0] = steps(v.tensor_tensor(Z[:, t, :], Z[:, t, :], scale_sb[:, :], ALU.mult))

            def rows_add(h):
                steps.need(rows_mark[0])
                for t in tiles_of(h):
                    rows_mark[0] = steps(v.tensor_tensor(X[:, t, :], X[:, t, :], Z[:, t, :], ALU.add))

            def rows_moments(h):
                steps.need(rows_mark[0])
                rows_mark[1] = norm_request(tiles_of(h), [X[:, t, :] for t in tiles_of(h)], 1.0, EPS)

            def rows_norm(h):
                r = rows_mark[1]
                dve.wait_ge(rstd_ready, r + 1)
                for k, t in enumerate(tiles_of(h)):
                    rows_mark[0] = steps(v.tensor_scalar(XN[:, t, :], X[:, t, :], mv[:, t, 0:1], rstd[:, r, k:k + 1],
                                                         ALU.subtract, ALU.mult))

            def rows_mix(h, term):
                steps.need(rows_mark[0])
                if term:
                    dve.wait_ge(sym_added, 2 * h + 2)
                for t in tiles_of(h):
                    rows_mark[0] = steps(v.scalar_tensor_tensor(X[:, t, :], (XN, SIM)[term][:, t, :],
                                                                k_mix[:, term:term + 1], X[:, t, :], ALU.mult, ALU.add))

            def top_find(h):
                for u in (2 * h, 2 * h + 1):
                    dve.wait_ge(x16hi_ready, u + 1)
                    a, z = (u % 2) * 256, (u % 2 + 1) * 256
                    v.tensor_tensor(x16[:, h, 1, :, a:z], xn_t[:, u % 2, :, :], x16[:, h, 0, :, a:z],
                                    ALU.subtract).then_inc(x16_ready, 1)
                dve.wait_ge(logits1_ready, h + 1)
                v.tensor_copy(lg[:, :, :], ps_prep[:, 0:320].rearrange("p (t n) -> p t n", t=HT)[:, :, 0:E1 + 1]
                              ).then_inc(logits1_copied, 1)
                dve.wait_ge(logits1_copied, h + 1)
                for k in range(HT):
                    m = steps(v.max(top[:, k, :], lg[:, k, 0:E1]))
                steps.need(m)
                v.tensor_scalar(nmax[:, HT * h:HT * h + HT], top[:, :, 0], -1.0, None, ALU.mult).then_inc(top_ready, 1)
                for k in range(HT):
                    top_mark[k] = steps(v.match_replace(rep[:, k, :], top[:, k, :], lg[:, k, 0:E1], NEG))

            top_mark = {}

            def top_weigh(h):
                tiles = tiles_of(h)
                a, z = tiles[0], tiles[-1] + 1
                for k, t in enumerate(tiles):
                    steps.need(top_mark[k])
                    dve.wait_ge(exp1_ready, t + 1)
                    m = steps(v.scalar_tensor_tensor(ex1[:, k, :], rep[:, k, :], NEG, ex1[:, k, :],
                                                     ALU.is_equal, ALU.mult, accum_out=den[:, t:t + 1]))
                m2 = steps(v.tensor_scalar(sgt[:, a:z], sgt[:, a:z], 0.5, 0.5, ALU.mult, ALU.add))
                steps.need(m2)
                m = steps(v.reciprocal(rden[:, a:z], den[:, a:z]))
                m2 = steps(v.tensor_copy(ws16[:, :, 0], sgt[:, a:z]))
                steps.need(m2)
                marks = [steps(v.tensor_scalar(w16[:, k, 0:E1], ex1[:, k, :], rden[:, t:t + 1], None, ALU.mult))
                         for k, t in enumerate(tiles)]
                steps(v.tensor_tensor(ws16[:, :, 1], sgt[:, a:z], ws16[:, :, 0], ALU.subtract))
                for k, t in enumerate(tiles):
                    steps.need(marks[k])
                    v.scalar_tensor_tensor(w16[:, k, E1:], ex1[:, k, :], rden[:, t:t + 1], w16[:, k, 0:E1],
                                           ALU.mult, ALU.subtract).then_inc(w16_ready, 1)

            r0, r1 = center(0), center(1)
            normalise(r0, 0, p_ready)
            normalise(r1, 1, p_ready)
            dve.wait_ge(w0_in, 16)
            steps(v.tensor_scalar(tern[:, :, :], w0_sb, 0.25, None, ALU.is_gt))
            m = steps(v.tensor_scalar(w0_sb, w0_sb, -0.25, None, ALU.is_lt))
            steps.need(m)
            v.tensor_tensor(tern[:, :, :], tern[:, :, :], w0_sb, ALU.subtract).then_inc(tern_set, 1)
            dve.wait_ge(norm_in, 16 * 2)
            similarity(0)
            dve.wait_ge(gates_done, 1)
            steps(v.tensor_scalar(k_mix[:, 2:3], tg[:, 4:5], -0.5, 0.5, ALU.mult, ALU.add))
            m = steps(v.tensor_scalar(k_mix[:, 3:4], tg[:, 4:5], 0.125, 0.125, ALU.mult, ALU.add))
            steps.need(m)
            steps(v.tensor_tensor(k_mix[:, 0:1], k_mix[:, 2:3], tg[:, 1:2], ALU.mult))
            steps(v.tensor_tensor(k_mix[:, 1:2], k_mix[:, 3:4], tg[:, 1:2], ALU.mult))
            split_done = attend(0)
            dve.wait_ge(const_set, 4)
            route(0, split_done)

            def clear(h):
                for k in range(HT):
                    i = v.memset(Z[:, HT * h + k, :], 0.0)
                    if h == 0:
                        i.then_inc(y_free, 1)
                    else:
                        last = steps(i)
                if h == 0:
                    dve.wait_ge(y_free, HT)
                else:
                    steps.need(last)

            clear(0)
            similarity(1)
            split_done = attend(1)
            experts0(0, 0)
            experts0(0, 1, find=0)
            route(1, split_done)
            experts0(0, 2, find=1)
            clear(1)
            experts0(0, 3, find=2)
            experts0(1, 0, find=3)
            experts0(1, 1)
            rows_scale(0)
            rows_sym(0, 0)
            rows_sym(0, 1)
            rows_add(0)
            rows_moments(0)
            rows_norm(0)
            rows_mix(0, 0)
            rows_mix(0, 1)
            rows_moments(0)
            normalise(rows_mark[1], 0, xn3_ready)
            experts0(1, 2)
            top_find(0)
            top_weigh(0)
            experts0(1, 3)

            NS = PAIRS + 1

            def gate_up(n, s, m=P, first=False):
                dve.wait_ge(up_ready, n + 1)
                dve.wait_ge(silu_ready, n + 1)
                v.tensor_tensor(gated[0:m, s, :], silu[0:m, s, :], ps_up[s][0:m, :], ALU.mult).then_inc(gated_ready, 1)
                dve.wait_ge(wb_ready, n + 1)
                dve.wait_ge(gated_ready, n + 1)
                if not first:
                    dve.wait_ge(ihi_ready, n - 1)
                v.tensor_tensor(inter[0:m, s, :], gated[0:m, s, :], ps_w[0:m, :], ALU.mult).then_inc(inter_ready, 1)

            def low_step(n, s, m=P):
                dve.wait_ge(inter_ready, n + 1)
                dve.wait_ge(ihi_ready, n + 1)
                v.tensor_tensor(inter16[0:m, s, 1, :], inter[0:m, s, :], inter16[0:m, s, 0, :], ALU.subtract
                                ).then_inc(ilo_ready, 1)

            def final(h):
                dve.wait_ge(down_ready, (h + 1) * NS)
                for k in range(HT):
                    t = HT * h + k
                    v.scalar_tensor_tensor(X[:, t, :], ps_down[k // 2][:, (k % 2) * D:(k % 2 + 1) * D], tg[:, 3:4],
                                           X[:, t, :], ALU.mult, ALU.add).then_inc(out_ready, 1)

            for n in range(NS):
                q, s, m = n - 1, (n + 1) % 2, I1 if n == 0 else P
                gate_up(n, s, m, first=(n < 2))
                t, i = HT + (q - 1) // 4, (q - 1) % 4 * 5
                finding = 1 <= q <= 4 * HT
                if finding:
                    find_top(t, i, i + 2)
                low_step(n, s, m)
                if finding:
                    find_top(t, i + 2, i + 5)
                    if q % 4 == 0:
                        adjacency(t)
                if q == 17:
                    rows_sym(1, 0)
                if q == 18:
                    rows_scale(1)
                if q == 19:
                    rows_sym(1, 1)
                if q == 20:
                    rows_add(1)
                if q == 21:
                    rows_moments(1)
                if q == 22:
                    rows_norm(1)
                if q == 23:
                    rows_mix(1, 0)
                if q == 24:
                    rows_mix(1, 1)
                if q == 25:
                    rows_moments(1)
                if q == 26:
                    normalise(rows_mark[1], 1, xn3_ready)
                if q == 27:
                    top_find(1)
                if q == 28:
                    top_weigh(1)
            final(0)
            gate_up(NS, 1, I1)
            low_step(NS, 1, I1)
            gate_up(NS + 1, 0)
            low_step(NS + 1, 0)
            with dve.Fori(0, (PAIRS - 2) // 2) as turn:
                for j in range(2):
                    n = turn * 2 + (NS + 2 + j)
                    gate_up(n, (1 + j) % 2)
                    low_step(n, (1 + j) % 2)
            gate_up(2 * NS - 1, 1)
            low_step(2 * NS - 1, 1)
            final(1)


def kernel(**inputs):
    import numpy as np
    import concourse.bacc as bacc
    from concourse.bass_utils import run_bass_kernel_spmd

    a = {k: np.asarray(w) for k, w in inputs.items()}
    laid = {
        "x": a["x"],
        "ctx_t": a["ctx_512"].reshape(B * S, DC).T,
        "g_xattn": a["g_xattn"], "g_ffn": a["g_ffn"],
        "wk_t": a["L0_xattn_W_k"].T, "b_k": a["L0_xattn_b_k"],
        "ln_gamma": a["L0_xattn_ln_gamma"], "ln_beta": a["L0_xattn_ln_beta"],
        "w0_t": a["L0_ffn_weight"].T, "scale0": a["L0_ffn_scale"],
        "masks_t": a["L0_ffn_expert_masks"].transpose(2, 0, 1).reshape(D, E0 // 2, 2 * D),
        "router_t": a["L0_ffn_router_w"].T,
        "wq1_t": a["L1_xattn_Wq"].T, "wk1_t": a["L1_xattn_Wk"].T,
        "gamma_raw": a["L1_xattn_gamma_raw"].reshape(1),
        "gate_t": a["L1_ffn_gate_w"].T,
        "gu_t": a["L1_ffn_gu_w"].reshape(PAIRS, 2, 2, I1, D).transpose(4, 0, 2, 1, 3).reshape(D, PAIRS, 4 * I1),
        "dp_t": a["L1_ffn_dp_w"].transpose(0, 2, 1).reshape(E1 * I1, D),
        "shg_t": a["L1_ffn_sh_gate_w"].T, "shu_t": a["L1_ffn_sh_up_w"].T,
        "shd_t": a["L1_ffn_sh_down_w"].T, "shgate_t": a["L1_ffn_sh_gate1_w"].T,
    }
    nc = bacc.Bacc("TRN2", target_bir_lowering=False, num_devices=1)
    arrays, args = {}, []
    for name, w in laid.items():
        w = np.ascontiguousarray(w)
        arrays[f"in_{name}"] = w
        args.append(nc.dram_tensor(f"in_{name}", w.shape, mybir.dt.from_np(w.dtype), kind="ExternalInput").ap())
    out = nc.dram_tensor("out", (B, S, D), F32, kind="ExternalOutput").ap()
    flamingo_block(nc, *args, out)
    r = run_bass_kernel_spmd(nc, [arrays], core_ids=[0])
    return r.results[0]["out"]
```

```python
from contextlib import ExitStack

import concourse.bass as bass
from concourse import mybir

ALU = mybir.AluOpType
ACT = mybir.ActivationFunctionType
F32 = mybir.dt.float32
F16 = mybir.dt.float16
U32 = mybir.dt.uint32
AX_X = mybir.AxisListType.X

P = 128
B, S, D = 4, 256, 256
DC = 64
T = B * S // P
HT = T // 2
HN = HT * P
C = D // P
E0 = 32
GR, MB = 4, 8
BP = MB // 2
E1, I1 = 64, 64
PAIRS = E1 // 2
NS = PAIRS + 1
WS = 4
TOPK = int(S * 0.3)
NEG = -3.0e38
EPS = 1e-5
EPS_SIM = 1e-6
SIM_SCALE = D ** -0.5
SIM1_SCALE = 1.0 / 16.0


class Steps:

    def __init__(self, engine, sem):
        self.engine, self.sem, self.n = engine, sem, 0

    def __call__(self, instruction):
        instruction.then_inc(self.sem, 1)
        self.n += 1
        return self.n

    def need(self, step):
        self.engine.wait_ge(self.sem, step)


def flamingo_block(nc, x, ctx_t, g_xattn, g_ffn, wk_t, b_k, ln_gamma, ln_beta, w0_t, scale0, masks_t,
                   router_t, wq1_t, wk1_t, gamma_raw, gate_t, gu_t, dp_t, shg_t, shu_t, shd_t, shgate_t, out):
    with ExitStack() as stack:
        def sb(name, shape, dt=F32):
            return stack.enter_context(nc.sbuf_tensor(name, shape, dt))

        def sem(name):
            return stack.enter_context(nc.semaphore(name))

        X = sb("X", [P, T, D])
        XN = sb("XN", [P, T, D])
        Z = sb("Z", [P, T, D])
        SIM = sb("SIM", [P, T, S])
        gu16 = sb("gu16", [P, PAIRS, 2, C, 256], F16)
        m16 = gu16[:, PAIRS // 2:, :, :, :].rearrange("p a b c d -> p (a b c d)").rearrange(
            "p (c e o) -> p c e o", c=C, e=E0)
        rows16 = gu16[:, 12:14, :, :, :].rearrange("p a b c d -> p (a b c d)").rearrange(
            "p (k s n) -> p k s n", k=HT, s=2)
        diag = gu16[:, 14:16, :, :, :].rearrange("p a b c d -> p (a b c d)").rearrange(
            "p (k g n) -> p k g n", k=HT, g=GR)
        stage_dp = sb("stage_dp", [P, 2 * C * GR * 2 * D])
        mask_stage = stage_dp[:, :].rearrange("p (s c a n) -> p s c a n", s=2, c=C, a=GR)
        dp16 = stage_dp[:, :].bitcast(F16).rearrange("p (q s n) -> p q s n", q=PAIRS, s=2)
        xg = sb("xg", [P, T, 2, C, GR * P], F16)
        act_area = xg[:, :, :, :, :].rearrange("p a b c d -> p (a b c d)")
        silu = act_area[:, 0:2048].bitcast(F32).rearrange("p (s n) -> p s n", s=2)
        gated = act_area[:, 2048:4096].bitcast(F32).rearrange("p (s n) -> p s n", s=2)
        inter = act_area[:, 4096:6144].bitcast(F32).rearrange("p (s n) -> p s n", s=2)
        inter16 = act_area[:, 6144:8192].rearrange("p (s h n) -> p s h n", s=2, h=2)
        stage = sb("stage", [P, 2, 768])
        early = sb("early", [P, 5120])
        ctx_sb = early[0:DC + 1, 0:1024]
        kv_t = early[0:DC, 1024:2048]
        kv = early[:, 2048:2560].rearrange("p (t d) -> p t d", d=DC)
        q_t = early[0:DC, 2560:3072]
        k_t = early[0:DC, 3072:3584]
        p_t = early[:, 3584:4608].rearrange("p (s c n) -> p s c n", s=2, c=C)
        o_t = early[0:DC, 4608:5120].rearrange("p (s n) -> p s n", s=2)
        late = early[:, :].bitcast(F16)
        x16 = late[:, 0:4096].rearrange("p (h s c n) -> p h s c n", h=2, s=2, c=C)
        w_rows = early[:, 2048:4096].rearrange("p (s n) -> p s n", s=WS)
        w_t = early[0:E1 + 1, 4096:5120].rearrange("p (h n) -> p h n", h=2)

        xn_t = sb("xn_t", [P, 2, C, 2 * P])
        gamma_sb = sb("gamma_sb", [P, S])
        beta_sb = sb("beta_sb", [P, S])
        scale_sb = sb("scale_sb", [P, D])
        ident = sb("ident", [P, P])
        ident16 = sb("ident16", [P, P], F16)
        iota = sb("iota", [P, E0])
        minus_half = sb("minus_half", [P, 4])
        wk_sb = sb("wk_sb", [DC + 1, DC])
        wqk_sb = sb("wqk_sb", [DC, 2 * DC])
        tern = sb("tern", [P, C, D])
        w0_sb = Z[:, 6:8, :]
        shared_stage = Z[:, 4, :].rearrange("p (c n) -> p c n", c=C)
        shared_dn_stage = Z[0:I1, 5, :]
        router_sb = sb("router_sb", [P, C, E0])
        gate_sb = sb("gate_sb", [P, C, E1 + 1])
        gates = sb("gates", [P, 5])
        tg = sb("tg", [P, 5])
        k_mix = sb("k_mix", [P, 4])
        shared16 = sb("shared16", [P, 2, C, 128], F16)
        shared_dn16 = sb("shared_dn16", [I1, 2, D], F16)
        bn = sb("bn", [P, T, 6])
        mv = sb("mv", [P, T, 2])
        NR = 10
        var_in = sb("var_in", [P, NR, 4])
        rstd = sb("rstd", [P, NR, 4])
        tiny = sb("tiny", [P, 8, T])
        c_mem = sb("c_mem", [P, T, MB])
        lg0 = sb("lg0", [P, HT, E0])
        oh = sb("oh", [P, HT, E0])
        ohw = sb("ohw", [P, HT, E0])
        grp = sb("grp", [P, HT, GR])
        m8i = sb("m8i", [P, HT, 8], U32)
        idxf = sb("idxf", [P, HT])
        work = sb("work", [P, S])
        t8 = sb("t8", [P, 8])
        lg = sb("lg", [P, HT, E1 + 1])
        rep = Z[:, 0, :].rearrange("p (t n) -> p t n", t=HT)
        ex1 = Z[:, 1, :].rearrange("p (t n) -> p t n", t=HT)
        w1 = Z[:, 2:4, :].rearrange("p a b -> p (a b)")[:, 0:HT * (E1 + 1)].rearrange("p (t n) -> p t n", t=HT)
        top = sb("top", [P, HT, 8])
        nmax, den, rden, r16, nm0, wtop, den1, sgt = (tiny[:, j, :] for j in range(8))

        bank = [stack.enter_context(nc.psum_tensor(f"bank{j}", [P, 512], F32)) for j in range(8)]
        ps_kv = [bank[3], bank[4]]
        ps_kvr = bank[5]
        ps_tr = bank[1]
        ps_small = bank[2]
        ps_sim = [bank[0], bank[7]]
        ps_sim1 = [bank[5], bank[6]]
        ps_y = [bank[3], bank[4], bank[5], bank[6]]

        def grp_bank(t, n):
            if t == 0:
                return bank[3 + n]
            return bank[((5, 6) if t < HT else (0, 7))[n]] if n < 2 else bank[n - 1]

        ps_sym = [bank[0], bank[1]], [bank[1], bank[2]]
        ps_gate = [bank[3], bank[4]]
        ps_up = [bank[5], bank[6]]
        ps_prep = bank[2]
        ps_x3t = [bank[2], bank[1]]
        ps_down = [bank[0], bank[7]]

        x_in = [sem(f"x_in{b}") for b in range(B)]
        ctx_in, attn_in, small_in = sem("ctx_in"), sem("attn_in"), sem("small_in")
        w0_in, norm_in, qk_in = sem("w0_in"), sem("norm_in"), sem("qk_in")
        gates_in, late_in = sem("gates_in"), sem("late_in")
        mask_in = [sem(f"mask_in{s}") for s in range(2)]
        stage_in = [sem(f"stage_in{s}") for s in range(2)]
        ones_set, const_set, tern_set = sem("ones_set"), sem("const_set"), sem("tern_set")
        pool_step, dve_step, act_step = sem("pool_step"), sem("dve_step"), sem("act_step")
        gates_done = sem("gates_done")
        var_ready, rstd_ready = sem("var_ready"), sem("rstd_ready")
        mask_ready = sem("mask_ready")
        proj_ready, proj_copied = sem("proj_ready"), sem("proj_copied")
        p_ready, pt_ready, pt_copied = sem("p_ready"), sem("pt_ready"), sem("pt_copied")
        o_ready, o_copied, sim_ready = sem("o_ready"), sem("o_copied"), sem("sim_ready")
        sim_used, z_ready, exp_ready = sem("sim_used"), sem("z_ready"), sem("exp_ready")
        sim1_ready, sim1_copied = sem("sim1_ready"), sem("sim1_copied")
        xn_ready, xnt_ready, xnt_copied = sem("xn_ready"), sem("xnt_ready"), sem("xnt_copied")
        logits_ready, max_ready, exp0_ready = sem("logits_ready"), sem("max_ready"), sem("exp0_ready")
        diag_ready, xg_ready, xg_copied = sem("diag_ready"), sem("xg_ready"), sem("xg_copied")
        y_ready, y_free = sem("y_ready"), sem("y_free")
        th_ready, adj_ready, sym_ready = sem("th_ready"), sem("adj_ready"), sem("sym_ready")
        hi_ready, lo_ready = sem("hi_ready"), sem("lo_ready")
        xn3_ready, x3t_ready, x3t_copied = sem("xn3_ready"), sem("x3t_ready"), sem("x3t_copied")
        x16hi_ready, x16_ready = sem("x16hi_ready"), sem("x16_ready")
        logits1_ready, top_ready, exp1_ready = sem("logits1_ready"), sem("top_ready"), sem("exp1_ready")
        w1_ready, wt_ready, wt_copied = sem("w1_ready"), sem("wt_ready"), sem("wt_copied")
        w_out, w_in = sem("w_out"), [sem(f"w_in{s}") for s in range(WS)]
        shared_hi, shared_set = sem("shared_hi"), sem("shared_set")
        gate_ready, up_ready = sem("gate_ready"), sem("up_ready")
        silu_ready, gated_ready, inter_ready = sem("silu_ready"), sem("gated_ready"), sem("inter_ready")
        ihi_ready, ilo_ready = sem("ihi_ready"), sem("ilo_ready")
        down_ready = sem("down_ready")
        out_ready, out_done = sem("out_ready"), sem("out_done")
        logits1_copied, sym_added = sem("logits1_copied"), sem("sym_added")

        x_d = x.rearrange("b s d -> (b s) d").rearrange("(t p) d -> p t d", p=P)
        out_d = out.rearrange("b s d -> (b s) d").rearrange("(t p) d -> p t d", p=P)
        mask_d = masks_t.rearrange("(c p) (a m) n -> p c a m n", p=P, a=GR)
        gu_d = gu_t.rearrange("(c p) q n -> p c q n", p=P)
        dp_d = dp_t.rearrange("(q p) n -> p q n", p=P)
        stage_gu = [stage[:, s, 0:512].rearrange("p (c n) -> p c n", c=C) for s in range(2)]
        stage_dn = [stage[:, s, 512:768] for s in range(2)]
        GC = C * GR

        w_d = nc.dram_tensor("token_weights", (2, E1 + 1, HN), F32).ap()

        block = stack.enter_context(nc.Block())

        @block.sync
        def _(sp):
            def load_row(dst, src, signal):
                sp.dma_start(dst, src.rearrange("(a d) -> a d", a=1).to_broadcast([P, src.shape[0]])
                             ).then_inc(signal, 16)

            for b in range(B):
                sp.dma_start(X[:, 2 * b:2 * b + 2, :], x_d[:, 2 * b:2 * b + 2, :]).then_inc(x_in[b], 16)
            sp.dma_start(w0_sb, w0_t.rearrange("(c p) n -> p c n", p=P)).then_inc(w0_in, 16)
            load_row(gamma_sb[:, :], ln_gamma, norm_in)
            load_row(beta_sb[:, :], ln_beta, norm_in)

            def load_masks(bp):
                if bp >= 2:
                    sp.wait_ge(mask_ready, GC * (bp - 1))
                for c in range(C):
                    sp.dma_start(mask_stage[:, bp % 2, c, :, :],
                                 mask_d[:, c, :, bp, :]).then_inc(mask_in[bp % 2], 16)

            load_masks(0)
            sp.dma_start(wqk_sb[:, 0:DC], wq1_t).then_inc(qk_in, 16)
            sp.dma_start(wqk_sb[:, DC:], wk1_t).then_inc(qk_in, 16)
            load_row(gates[:, 0:2], g_xattn, gates_in)
            load_row(gates[:, 2:4], g_ffn, gates_in)
            load_row(gates[:, 4:5], gamma_raw, gates_in)
            sp.dma_start(router_sb[:, :, :], router_t.rearrange("(c p) n -> p c n", p=P)).then_inc(small_in, 16)
            sp.dma_start(shared_stage[:, :, 0:I1], shg_t.rearrange("(c p) n -> p c n", p=P)).then_inc(small_in, 16)
            sp.dma_start(shared_stage[:, :, I1:128], shu_t.rearrange("(c p) n -> p c n", p=P)).then_inc(small_in, 16)
            sp.dma_start(shared_dn_stage, shd_t).then_inc(small_in, 16)
            load_masks(1)
            sp.dma_start(gate_sb[:, :, 0:E1], gate_t.rearrange("(c p) n -> p c n", p=P)).then_inc(late_in, 16)
            sp.dma_start(gate_sb[:, 0, E1:E1 + 1], shgate_t[0:P, :]).then_inc(late_in, 16)
            sp.dma_start(gate_sb[:, 1, E1:E1 + 1], shgate_t[P:D, :]).then_inc(late_in, 16)
            load_row(scale_sb[:, :], scale0, late_in)
            load_masks(2)
            load_masks(3)

            def load_pair(q, s):
                sp.dma_start(stage_gu[s], gu_d[:, :, bass.ds(q, 1), :].rearrange("p c q n -> p c (q n)")
                             ).then_inc(stage_in[s], 16)
                sp.dma_start(stage_dn[s], dp_d[:, bass.ds(q, 1), :].rearrange("p q n -> p (q n)")
                             ).then_inc(stage_in[s], 16)

            load_pair(0, 0)
            load_pair(1, 1)

            def load_pairs(lo, hi):
                with sp.Fori(0, (hi - lo) // 2) as turn:
                    q = turn * 2 + lo
                    for s in range(2):
                        sp.wait_ge(lo_ready, q + (s - 1))
                        load_pair(q + s, s)

            def write_weights(h):
                sp.wait_ge(wt_copied, h + 1)
                sp.dma_start(w_d[h, :, :], w_t[:, h, :]).then_inc(w_out, 16)

            def load_weights(h, n, slot):
                if isinstance(n, int) and n % NS == 0:
                    for e in range(2):
                        sp.dma_start(w_rows[e * I1 // 2:(e + 1) * I1 // 2, slot, :],
                                     w_d[h, E1:E1 + 1, :].to_broadcast([I1 // 2, HN])).then_inc(w_in[slot], 16)
                else:
                    for e in range(2):
                        row = w_d[h, bass.ds(n * 2 + (e - 2 - 2 * NS * h), 1), :]
                        sp.dma_start(w_rows[e * I1:(e + 1) * I1, slot, :], row.to_broadcast([I1, HN])
                                     ).then_inc(w_in[slot], 16)

            def next_weights(h, n, slot):
                sp.wait_ge(inter_ready, n - (WS - 1))
                load_weights(h, n, slot)

            load_pairs(2, PAIRS // 2)
            write_weights(0)
            sp.wait_ge(w_out, 16)
            for n in range(WS):
                load_weights(0, n, n)
            with sp.Fori(0, PAIRS // 2 // WS) as turn:
                for j in range(WS):
                    next_weights(0, turn * WS + (WS + j), j)
                    sp.wait_ge(lo_ready, turn * WS + (PAIRS // 2 - 1 + j))
                    load_pair(turn * WS + (PAIRS // 2 + j), j % 2)
            with sp.Fori(0, (NS - WS - PAIRS // 2) // WS) as turn:
                for j in range(WS):
                    next_weights(0, turn * WS + (WS + PAIRS // 2 + j), j)
            next_weights(0, NS - 1, (NS - 1) % WS)
            write_weights(1)
            sp.wait_ge(w_out, 16 * 2)
            for n in range(NS, NS + WS - 1):
                next_weights(1, n, n % WS)
            with sp.Fori(0, (NS - WS + 1) // WS) as turn:
                for j in range(WS):
                    next_weights(1, turn * WS + (NS + WS - 1 + j), j)
            for n in range(2 * NS - 2, 2 * NS):
                next_weights(1, n, n % WS)
            for t in range(T):
                sp.wait_ge(out_ready, t + 1)
                sp.dma_start(out_d[:, t, :], X[:, t, :]).then_inc(out_done, 16)
            sp.wait_ge(out_done, 16 * T)

        @block.gpsimd
        def _(pool):
            steps = Steps(pool, pool_step)
            nc.gpsimd.memset(ctx_sb[DC:DC + 1, :], 1.0).then_inc(ones_set, 1)
            pool.wait_ge(ones_set, 1)
            nc.gpsimd.memset(minus_half[:, :], -0.5).then_inc(const_set, 1)
            a = steps(nc.gpsimd.memset(ident[:, :], 0.0))
            b16 = steps(nc.gpsimd.memset(ident16[:, :], 0.0))
            for ready, m in ((a, ident), (b16, ident16)):
                steps.need(ready)
                nc.gpsimd.affine_select(out=m[:, :], in_=m[:, :], compare_op=ALU.not_equal, fill=1.0, base=0,
                                        pattern=[[-1, P]], channel_multiplier=1).then_inc(const_set, 1)
            nc.gpsimd.iota(iota[:, :], pattern=[[1, E0]], base=0, channel_multiplier=0,
                           allow_small_or_imprecise_dtypes=True).then_inc(const_set, 1)
            pool.wait_ge(const_set, 1)

            def rsqrt(r, n):
                pool.wait_ge(var_ready, r + 1)
                nc.gpsimd.tensor_tensor(rstd[:, r, 0:n], var_in[:, r, 0:n], minus_half[:, 0:n],
                                        ALU.pow).then_inc(rstd_ready, 1)

            def mask_piece(n):
                bp, c, g = n // (C * GR), n // GR % C, n % GR
                if n == 0:
                    pool.wait_ge(tern_set, 1)
                if n % (C * GR) == 0:
                    pool.wait_ge(mask_in[bp % 2], 16 * C * (bp // 2 + 1))
                e = g * MB + 2 * bp
                for m in range(2):
                    last = nc.gpsimd.tensor_tensor(m16[:, c, e + m, :], mask_stage[:, bp % 2, c, g, m * D:(m + 1) * D],
                                                   tern[:, c, :], ALU.mult)
                last.then_inc(mask_ready, 1)

            upto = (0, 3, 11, 22, 30, GC * BP)
            done = 0
            for r in range(6):
                rsqrt(r, HT)
                for n in range(done, upto[r]):
                    mask_piece(n)
                    if n == 13:
                        pool.wait_ge(shared_hi, 2)
                        nc.gpsimd.tensor_tensor(shared16[:, 1, :, :], shared_stage, shared16[:, 0, :, :],
                                                ALU.subtract).then_inc(shared_set, 1)
                        nc.gpsimd.tensor_tensor(shared_dn16[:, 1, :], shared_dn_stage, shared_dn16[:, 0, :],
                                                ALU.subtract).then_inc(shared_set, 1)
                done = upto[r]

            def low_half(q, s):
                pool.wait_ge(hi_ready, q + 1)
                nc.gpsimd.tensor_tensor(gu16[:, bass.ds(q, 1), 1, :, :].rearrange("p q c n -> p (q c) n"),
                                        stage_gu[s], gu16[:, bass.ds(q, 1), 0, :, :].rearrange("p q c n -> p (q c) n"),
                                        ALU.subtract)
                nc.gpsimd.tensor_tensor(dp16[:, bass.ds(q, 1), 1, :].rearrange("p q n -> p (q n)"), stage_dn[s],
                                        dp16[:, bass.ds(q, 1), 0, :].rearrange("p q n -> p (q n)"),
                                        ALU.subtract).then_inc(lo_ready, 1)

            with pool.Fori(0, (PAIRS // 2 - 0) // 2) as turn:
                q = turn * 2 + 0
                for s in range(2):
                    low_half(q + s, s)
            rsqrt(6, HT)
            rsqrt(7, HT)
            with pool.Fori(0, (PAIRS - PAIRS // 2) // 2) as turn:
                q = turn * 2 + PAIRS // 2
                for s in range(2):
                    low_half(q + s, s)
            rsqrt(8, HT)
            rsqrt(9, HT)

        @block.scalar
        def _(act):
            def copy(dst, src, scale=1.0):
                return nc.scalar.activation(dst, src, ACT.Copy, scale=scale)

            act.dma_start(ctx_sb[0:DC, :], ctx_t).then_inc(ctx_in, 16)
            act.dma_start(wk_sb[0:DC, :], wk_t).then_inc(attn_in, 16)
            act.dma_start(wk_sb[DC:DC + 1, :], b_k.rearrange("(a d) -> a d", a=1)).then_inc(attn_in, 16)

            for h in range(2):
                act.wait_ge(proj_ready, h + 1)
                copy(kv_t[:, h * 512:(h + 1) * 512], ps_kv[h][0:DC, :]).then_inc(proj_copied, 1)
            act.wait_ge(proj_ready, 3)
            copy(kv[:, :, :].rearrange("p t d -> p (t d)"), ps_kvr[:, :]).then_inc(proj_copied, 1)

            def attention_rows(b):
                act.wait_ge(pt_ready, b + 1)
                if b >= 2:
                    act.wait_ge(o_ready, b - 1)
                copy(p_t[:, b % 2, :, :].rearrange("p c n -> p (c n)"), ps_tr[:, :]).then_inc(pt_copied, 1)
                act.wait_ge(o_ready, b + 1)
                if b >= 2:
                    act.wait_ge(sim_ready, b - 1)
                copy(o_t[:, b % 2, :], ps_small[0:DC, 0:256]).then_inc(o_copied, 1)

            def softmax_rows(h):
                for t in range(HT * h, HT * h + HT):
                    act.wait_ge(z_ready, h + 1)
                    nc.scalar.activation(Z[:, t, :], Z[:, t, :], ACT.Exp, bias=nmax[:, t:t + 1],
                                         accum_out=den[:, t:t + 1]).then_inc(exp_ready, 1)

            def qk_rows(h):
                for j, dst in enumerate((q_t, k_t)):
                    act.wait_ge(proj_ready, 4 + h)
                    copy(dst, ps_kv[h][j * DC:(j + 1) * DC, :]).then_inc(proj_copied, 1)

            def sim1_rows(h):
                for k in range(2):
                    act.wait_ge(sim1_ready, 2 * h + k + 1)
                    t = 4 * h + 2 * k
                    copy(SIM[:, t:t + 2, :].rearrange("p t n -> p (t n)"), ps_sim1[k][:, :],
                         SIM1_SCALE).then_inc(sim1_copied, 1)

            attention_rows(0)
            attention_rows(1)
            act.wait_ge(gates_in, 16 * 3)
            nc.scalar.activation(tg[:, 0:4], gates[:, 0:4], ACT.Tanh).then_inc(act_step, 1)
            nc.scalar.activation(tg[:, 4:5], gates[:, 4:5], ACT.Tanh, scale=0.5).then_inc(gates_done, 1)
            qk_rows(0)
            sim1_rows(0)
            attention_rows(2)
            softmax_rows(0)
            attention_rows(3)
            qk_rows(1)
            act.wait_ge(small_in, 16 * 4)
            copy(shared16[:, 0, :, :], shared_stage).then_inc(shared_hi, 1)
            copy(shared_dn16[:, 0, :], shared_dn_stage).then_inc(shared_hi, 1)

            def router_rows(h):
                for u in (2 * h, 2 * h + 1):
                    act.wait_ge(xnt_ready, u + 1)
                    if u >= 2:
                        act.wait_ge(logits_ready, h)
                    copy(xn_t[:, u % 2, :, :].rearrange("p c n -> p (c n)"), ps_tr[:, :]).then_inc(xnt_copied, 1)

            def router_exp(h):
                act.wait_ge(max_ready, h + 1)
                for t in range(HT * h, HT * h + HT):
                    last = nc.scalar.activation(ohw[:, t % HT, :], lg0[:, t % HT, :], ACT.Exp, bias=nm0[:, t:t + 1],
                                                accum_out=den1[:, t:t + 1])
                last.then_inc(exp0_ready, 1)

            def grouped(t):
                for n in range(2 * C):
                    act.wait_ge(xg_ready, 2 * C * t + n + 1)
                    copy(xg[:, t, n // C, n % C, :], grp_bank(t, n)[:, :]).then_inc(xg_copied, 1)

            def tanh_rows(h):
                rows = XN[:, HT * h:HT * h + HT, :].rearrange("p t n -> p (t n)")
                nc.scalar.activation(rows, SIM[:, HT * h:HT * h + HT, :].rearrange("p t n -> p (t n)"), ACT.Tanh,
                                     scale=0.5).then_inc(act_step, 1)
                act.wait_ge(act_step, h + 2)
                nc.scalar.activation(rows, rows, ACT.Copy, bias=1.0).then_inc(th_ready, 1)

            def high_half(q, s, turn):
                act.wait_ge(stage_in[s], turn)
                copy(gu16[:, bass.ds(q, 1), 0, :, :].rearrange("p q c n -> p (q c) n"), stage_gu[s])
                copy(dp16[:, bass.ds(q, 1), 0, :].rearrange("p q n -> p (q n)"), stage_dn[s]).then_inc(hi_ready, 1)

            def high_halves(lo, hi):
                with act.Fori(0, (hi - lo) // 2) as turn:
                    for s in range(2):
                        high_half(turn * 2 + (lo + s), s, turn * 32 + (lo * 16 + 32))

            router_rows(0)
            sim1_rows(1)
            router_exp(0)
            for t in range(HT - 1):
                grouped(t)
            softmax_rows(1)
            grouped(HT - 1)
            tanh_rows(0)
            act.wait_ge(mask_ready, GC * BP)
            high_halves(0, 2)
            router_rows(1)
            router_exp(1)
            high_halves(2, 4)
            grouped(HT)
            grouped(HT + 1)
            high_halves(4, 6)
            grouped(HT + 2)
            grouped(HT + 3)
            tanh_rows(1)
            high_halves(6, 16)

            def prep_rows(h):
                for u in (2 * h, 2 * h + 1):
                    act.wait_ge(x3t_ready, u + 1)
                    if u >= 2:
                        act.wait_ge(x16_ready, u - 1)
                        act.wait_ge(logits1_ready, h)
                    copy(xn_t[:, u % 2, :, :].rearrange("p c n -> p (c n)"), ps_x3t[u % 2][:, :]).then_inc(x3t_copied, 1)
                    act.wait_ge(x3t_copied, u + 1)
                    copy(x16[:, h, 0, :, (u % 2) * 256:(u % 2 + 1) * 256], xn_t[:, u % 2, :, :]).then_inc(x16hi_ready, 1)

            def top_rows(h):
                for t in range(4 * h, 4 * h + 4):
                    act.wait_ge(top_ready, h + 1)
                    nc.scalar.activation(ex1[:, t % HT, :], lg[:, t % HT, 0:E1], ACT.Exp, bias=nmax[:, t:t + 1])
                    nc.scalar.activation(sgt[:, t:t + 1], lg[:, t % HT, E1:E1 + 1], ACT.Tanh,
                                         scale=0.5).then_inc(exp1_ready, 1)

            def prep_weights(h):
                act.wait_ge(wt_ready, h + 1)
                copy(w_t[:, h, :], ps_prep[0:E1 + 1, :]).then_inc(wt_copied, 1)

            prep_rows(0)
            top_rows(0)
            prep_weights(0)
            def silu_step(n, s, m=P):
                act.wait_ge(gate_ready, n + 1)
                act.wait_ge(gated_ready, n - 1)
                nc.scalar.activation(silu[0:m, s, :], ps_gate[s][0:m, :], ACT.Silu).then_inc(silu_ready, 1)

            def high_step(n, s):
                act.wait_ge(inter_ready, n + 1)
                act.wait_ge(down_ready, n - 1)
                copy(inter16[:, s, 0, :], inter[:, s, :]).then_inc(ihi_ready, 1)

            for h in range(2):
                b0 = h * NS
                for n in (0, 1):
                    s = (n + 1 + h) % 2
                    act.wait_ge(gate_ready, b0 + n + 1)
                    if b0 + n >= 2:
                        act.wait_ge(gated_ready, b0 + n - 1)
                    m = I1 if n == 0 else P
                    nc.scalar.activation(silu[0:m, s, :], ps_gate[s][0:m, :], ACT.Silu).then_inc(silu_ready, 1)
                    act.wait_ge(inter_ready, b0 + n + 1)
                    if b0 + n >= 2:
                        act.wait_ge(down_ready, b0 + n - 1)
                    copy(inter16[0:m, s, 0, :], inter[0:m, s, :]).then_inc(ihi_ready, 1)

                def pair_steps(lo, hi, convert=False):
                    def two(q):
                        for j in range(2):
                            s = (1 + j + h) % 2
                            silu_step(q + (b0 + 1 + j), s)
                            high_step(q + (b0 + 1 + j), s)
                            if convert:
                                high_half(q + (PAIRS // 2 - 1 + j), j, q * 16 + (16 * (PAIRS // 2 - 1) + 32))
                    with act.Fori(0, (hi - lo) // 2) as turn:
                        two(turn * 2 + lo)

                def one(q):
                    silu_step(b0 + 1 + q, (q + h) % 2)
                    high_step(b0 + 1 + q, (q + h) % 2)

                if h == 0:
                    pair_steps(1, 17, convert=True)
                    pair_steps(17, 25)
                    one(25)
                    one(26)
                    prep_rows(1)
                    one(27)
                    one(28)
                    top_rows(1)
                    one(29)
                    one(30)
                else:
                    pair_steps(1, 31)
                silu_step(b0 + PAIRS, 1 - h)
                if h == 0:
                    prep_weights(1)
                high_step(b0 + PAIRS, 1 - h)

        @block.tensor
        def _(pe):
            mm = nc.tensor.matmul

            pe.wait_ge(ones_set, 1)
            pe.wait_ge(ctx_in, 16)
            pe.wait_ge(attn_in, 32)
            for h in range(2):
                mm(ps_kv[h][0:DC, :], wk_sb[:, :], ctx_sb[:, h * 512:(h + 1) * 512], start=True, stop=True
                   ).then_inc(proj_ready, 1)
            pe.wait_ge(const_set, 4)
            for t in range(T):
                pe.wait_ge(proj_copied, t // HT + 1)
                last = nc.tensor.transpose(ps_kvr[:, t * DC:(t + 1) * DC], kv_t[:, t * P:(t + 1) * P],
                                           ident[0:DC, 0:DC])
            last.then_inc(proj_ready, 1)

            def transpose_p(b):
                pe.wait_ge(p_ready, 2 * b + 2)
                if b >= 1:
                    pe.wait_ge(pt_copied, b)
                for c in range(C):
                    for k in range(2):
                        last = nc.tensor.transpose(ps_tr[:, c * 256 + k * P:c * 256 + (k + 1) * P],
                                                   XN[:, 2 * b + k, c * P:(c + 1) * P], ident[:, :])
                last.then_inc(pt_ready, 1)

            def out_and_sim(b):
                pe.wait_ge(pt_copied, b + 1)
                pe.wait_ge(proj_copied, 3)
                if b >= 1:
                    pe.wait_ge(o_copied, b)
                for c in range(C):
                    last = mm(ps_small[0:DC, 0:256], kv[:, 2 * b + c, :], p_t[:, b % 2, c, :],
                              start=(c == 0), stop=(c == C - 1))
                last.then_inc(o_ready, 1)
                if b == 0:
                    transpose_p(1)
                if b == 2:
                    transpose_p(3)
                pe.wait_ge(o_copied, b + 1)
                if b >= 2:
                    pe.wait_ge(sim_used, 2 * (b - 1))
                for k in range(2):
                    last = mm(ps_sim[b % 2][:, k * 256:(k + 1) * 256], o_t[:, b % 2, k * P:(k + 1) * P],
                              kv_t[:, b * S:(b + 1) * S], start=True, stop=True)
                last.then_inc(sim_ready, 1)

            transpose_p(0)
            out_and_sim(0)
            out_and_sim(1)

            def qk(h):
                pe.wait_ge(qk_in, 32)
                mm(ps_kv[h][:, :], wqk_sb[:, :], ctx_sb[0:DC, h * 512:(h + 1) * 512], start=True, stop=True
                   ).then_inc(proj_ready, 1)

            def sim1(h):
                pe.wait_ge(proj_copied, 5 + 2 * h)
                for k in range(2):
                    if h == 1:
                        pe.wait_ge(sim1_copied, k + 1)
                    for i in range(2):
                        last = mm(ps_sim1[k][:, i * 256:(i + 1) * 256], q_t[:, k * S + i * P:k * S + (i + 1) * P],
                                  k_t[:, k * S:(k + 1) * S], start=True, stop=True)
                    last.then_inc(sim1_ready, 1)

            qk(0)
            sim1(0)
            transpose_p(2)
            out_and_sim(2)
            out_and_sim(3)
            qk(1)

            def router_x(us):
                for u in us:
                    pe.wait_ge(xn_ready, 2 * u + 2)
                    if u == 0:
                        pe.wait_ge(pt_copied, B)
                    else:
                        pe.wait_ge(xnt_copied, u)
                    for c in range(C):
                        for k in range(2):
                            last = nc.tensor.transpose(ps_tr[:, c * 256 + k * P:c * 256 + (k + 1) * P],
                                                       XN[:, 2 * u + k, c * P:(c + 1) * P], ident[:, :])
                    last.then_inc(xnt_ready, 1)

            def router(h):
                pe.wait_ge(xnt_copied, 2 * h + 2)
                if h == 0:
                    pe.wait_ge(o_copied, B)
                else:
                    pe.wait_ge(max_ready, 1)
                for k in range(HT):
                    for c in range(C):
                        last = mm(ps_small[:, k * E0:(k + 1) * E0], xn_t[:, k // 2, c, (k % 2) * P:(k % 2 + 1) * P],
                                  router_sb[:, c, :], start=(c == 0), stop=(c == C - 1))
                last.then_inc(logits_ready, 1)

            def group_rows(t):
                pe.wait_ge(diag_ready, t + 1)
                for n in range(2 * C):
                    if t == 0:
                        pe.wait_ge(sim1_copied, B)
                        pe.wait_ge(proj_copied, 7)
                    elif t == 1:
                        if n < 2:
                            pe.wait_ge(xg_copied, n + 3)
                        else:
                            pe.wait_ge(max_ready, 1)
                    elif t == HT:
                        if n < 2:
                            pe.wait_ge(sim_used, T)
                        else:
                            pe.wait_ge(max_ready, 2)
                    else:
                        pe.wait_ge(xg_copied, 2 * C * (t - 1) + n + 1)
                    mm(grp_bank(t, n)[:, :], rows16[:, t % 4, n // C, (n % C) * P:(n % C + 1) * P],
                       diag[:, t % HT, :, :].rearrange("p a n -> p (a n)"), start=True, stop=True
                       ).then_inc(xg_ready, 1)

            pe.wait_ge(small_in, 16 * 4)
            router_x((0, 1))
            router(0)
            sim1(1)
            group_rows(0)
            group_rows(1)

            def experts0(h, bp, after={}, before={}):
                pe.wait_ge(mask_ready, bp * (C * GR) + C * GR if h == 0 else C * GR * BP)
                for k in range(HT):
                    if k in before:
                        before[k]()
                    pe.wait_ge(y_free, bp * HT + (h * BP * HT + k + 1))
                    n = 0
                    for s in range(2):
                        for c in range(C):
                            for g in range(GR):
                                last = mm(ps_y[k][:, :], xg[:, HT * h + k, s, c, g * P:(g + 1) * P],
                                          m16[:, c, bass.ds(bp * 2 + g * MB, 2), :].rearrange("p e o -> p (e o)"),
                                          start=(n == 0), stop=(n == 2 * C * GR - 1))
                                n += 1
                    last.then_inc(y_ready, 1)
                    if k in after:
                        after[k]()

            def symmetric(h, which=None):
                for k in (0, 1) if which is None else (which,):
                    pe.wait_ge(adj_ready, 4 * h + 2 * k + 2)
                    dst = ps_sym[h][k]
                    if h == 1:
                        pe.wait_ge(wt_copied, 1)
                        pe.wait_ge(x3t_copied, 2)
                    for i in range(2):
                        for j in range(2):
                            last = nc.tensor.transpose(dst[:, i * 256 + j * P:i * 256 + (j + 1) * P],
                                                       SIM[:, 4 * h + 2 * k + j, i * P:(i + 1) * P], ident[:, :])
                    last.then_inc(sym_ready, 1)

            def prep_x3t(h):
                for u in (2 * h, 2 * h + 1):
                    pe.wait_ge(xn3_ready, 2 * u + 2)
                    if u == 2:
                        pe.wait_ge(sym_added, 4)
                    if u == 1:
                        pe.wait_ge(sym_added, 2)
                    for c in range(C):
                        for k in range(2):
                            last = nc.tensor.transpose(ps_x3t[u % 2][:, c * 256 + k * P:c * 256 + (k + 1) * P],
                                                       XN[:, 2 * u + k, c * P:(c + 1) * P], ident[:, :])
                    last.then_inc(x3t_ready, 1)

            def prep_logits(h):
                pe.wait_ge(x3t_copied, 2 * h + 2)
                pe.wait_ge(late_in, 16 * 4)
                for k in range(HT):
                    for c in range(C):
                        last = mm(ps_prep[:, k * 80:k * 80 + E1 + 1], xn_t[:, k // 2, c, (k % 2) * P:(k % 2 + 1) * P],
                                  gate_sb[:, c, :], start=(c == 0), stop=(c == C - 1))
                last.then_inc(logits1_ready, 1)

            def prep_wt(h):
                pe.wait_ge(w1_ready, HT * h + HT)
                for k in range(HT):
                    last = nc.tensor.transpose(ps_prep[0:E1 + 1, k * P:(k + 1) * P], w1[:, k, :], ident[:, :])
                last.then_inc(wt_ready, 1)

            def rows_behind(t):
                return lambda: group_rows(t)

            def copied(n):
                return lambda: pe.wait_ge(xg_copied, n)

            experts0(0, 0, {0: rows_behind(2), 1: rows_behind(3)},
                     {0: copied(2 * C), 1: copied(2 * 2 * C), 2: copied(2 * C * HT)})
            experts0(0, 1, {2: lambda: router_x((2,)), 3: lambda: router_x((3,))})
            experts0(0, 2, {0: lambda: router(1), 2: rows_behind(HT), 3: rows_behind(HT + 1)})
            experts0(0, 3, {0: rows_behind(HT + 2), 1: rows_behind(HT + 3)})
            pe.wait_ge(xg_copied, 2 * C * T)
            experts0(1, 0)
            experts0(1, 1, {1: lambda: symmetric(0)})
            experts0(1, 2, {2: lambda: prep_x3t(0), 3: lambda: prep_logits(0)})
            experts0(1, 3, {3: lambda: prep_wt(0)})

            SPLIT = ((0, 0), (0, 1), (1, 0))

            def project(n, s, q, h, m=P, before_up=None):
                for part, (dst, ready) in enumerate(((ps_gate[s], gate_ready), (ps_up[s], up_ready))):
                    if part and before_up is not None:
                        before_up()
                    k = 0
                    for a, b in SPLIT:
                        for c in range(C):
                            if q is None:
                                w = shared16[:, a, c, part * I1:(part + 1) * I1]
                            else:
                                w = gu16[:, bass.ds(q, 1), a, c, part * P:(part + 1) * P].rearrange("p q n -> p (q n)")
                            last = mm(dst[0:m, :], w, x16[:, h, b, c, :], start=(k == 0), stop=(k == 3 * C - 1))
                            k += 1
                    last.then_inc(ready, 1)

            def down(n, s, q, m=P):
                pe.wait_ge(ilo_ready, n + 1)
                for k in range(HT):
                    dst = ps_down[k // 2][:, (k % 2) * D:(k % 2 + 1) * D]
                    for j, (a, b) in enumerate(SPLIT):
                        if q is None:
                            w = shared_dn16[:, b, :]
                        else:
                            w = dp16[:, bass.ds(q, 1), b, :].rearrange("p q n -> p (q n)")
                        last = mm(dst, inter16[0:m, s, a, k * P:(k + 1) * P], w,
                                  start=(q is None and j == 0 and k % 2 == 0), stop=True, skip_group_check=True)
                last.then_inc(down_ready, 1)

            def slots_free(n):
                pe.wait_ge(silu_ready, n - 1)
                pe.wait_ge(gated_ready, n - 1)

            def shared_step(h):
                pe.wait_ge(x16_ready, 2 * h + 2)
                if h == 0:
                    pe.wait_ge(shared_set, 2)
                    pe.wait_ge(y_free, HT + 2 * BP * HT - 2)
                    project(0, 1, None, 0, I1, lambda: pe.wait_ge(y_free, HT + 2 * BP * HT))
                else:
                    slots_free(NS)
                    project(NS, 0, None, 1, I1)

            def pair_step(h, q, j):
                if h == 0:
                    pe.wait_ge(lo_ready, q + (j + 1))
                if not (h == 0 and isinstance(q, int) and q + j == 0):
                    slots_free(q + (h * NS + 1 + j))
                project(q + (h * NS + 1 + j), (j + h) % 2, q + j, h)

            def pair_steps(h, lo, hi):
                with pe.Fori(0, (hi - lo) // 2) as turn:
                    for j in range(2):
                        pair_step(h, turn * 2 + lo, j)
                        down(turn * 2 + (h * NS + lo - 1 + j), (j + h) % 2, turn * 2 + (lo - 2 + j))

            shared_step(0)
            pair_step(0, 0, 0)
            pair_step(0, 0, 1)
            down(0, 1, None, I1)
            pair_steps(0, 2, 16)
            symmetric(1, 0)
            pair_steps(0, 16, 18)
            symmetric(1, 1)
            pair_steps(0, 18, 26)
            pair_step(0, 26, 0)
            down(25, 0, 24)
            prep_x3t(1)
            pair_step(0, 26, 1)
            prep_logits(1)
            down(26, 1, 25)
            pair_steps(0, 28, 30)
            pair_step(0, 30, 0)
            down(29, 0, 28)
            pair_step(0, 30, 1)
            prep_wt(1)
            down(30, 1, 29)
            shared_step(1)
            down(31, 0, 30)
            pair_step(1, 0, 0)
            down(32, 1, 31)
            pair_step(1, 0, 1)
            pe.wait_ge(out_ready, HT)
            down(NS, 0, None, I1)
            pair_steps(1, 2, PAIRS)
            down(2 * NS - 2, 1, 30)
            down(2 * NS - 1, 0, 31)

        @block.vector
        def _(dve):
            v = nc.vector
            steps = Steps(dve, dve_step)
            asked = [0]

            def moments(src, t):
                return v.bn_stats(bn[:, t, :], src)

            def norm_request(tiles, sources, mul, eps, wait=lambda t: None):
                r = asked[0]
                asked[0] += 1
                marks = []
                for t, src in zip(tiles, sources):
                    wait(t)
                    marks.append(steps(moments(src, t)))
                for t, m in zip(tiles, marks):
                    steps.need(m)
                    m = steps(v.bn_aggr(mv[:, t, :], bn[:, t, :]))
                steps.need(m)
                v.tensor_scalar(var_in[:, r, 0:len(tiles)], mv[:, tiles[0]:tiles[-1] + 1, 1], mul, eps,
                                ALU.mult, ALU.add).then_inc(var_ready, 1)
                return r

            def tiles_of(h):
                return list(range(HT * h, HT * h + HT))

            def center(h):
                tiles = tiles_of(h)
                return norm_request(tiles, [X[:, t, :] for t in tiles], 1.0, EPS,
                                    wait=lambda t: dve.wait_ge(x_in[t // 2], 16))

            def normalise(r, h, ready):
                dve.wait_ge(rstd_ready, r + 1)
                for k, t in enumerate(tiles_of(h)):
                    v.tensor_scalar(XN[:, t, :], X[:, t, :], mv[:, t, 0:1], rstd[:, r, k:k + 1],
                                    ALU.subtract, ALU.mult).then_inc(ready, 1)

            def sim_bank(t):
                return ps_sim[t // 2 % 2][:, (t % 2) * 256:(t % 2 + 1) * 256]

            def similarity(h):
                tiles = tiles_of(h)
                r = norm_request(tiles, [sim_bank(t) for t in tiles], SIM_SCALE * SIM_SCALE, EPS_SIM,
                                 wait=lambda t: dve.wait_ge(sim_ready, t // 2 + 1))
                dve.wait_ge(rstd_ready, r + 1)
                a, z = tiles[0], tiles[-1] + 1
                m = steps(v.tensor_scalar(r16[:, a:z], rstd[:, r, :], SIM_SCALE, None, ALU.mult))
                if h == 1:
                    dve.wait_ge(shared_set, 2)
                for t in tiles:
                    v.scalar_tensor_tensor(Z[:, t, :], sim_bank(t), mv[:, t, 0:1], gamma_sb[:, :],
                                           ALU.subtract, ALU.mult).then_inc(sim_used, 1)
                steps.need(m)
                marks = []
                for t in tiles:
                    dve.wait_ge(sim_used, t + 1)
                    marks.append(steps(v.scalar_tensor_tensor(Z[:, t, :], Z[:, t, :], r16[:, t:t + 1], beta_sb[:, :],
                                                              ALU.mult, ALU.add)))
                for i, t in enumerate(tiles):
                    steps.need(marks[i])
                    m = steps(v.tensor_reduce(rden[:, t:t + 1], Z[:, t, :], AX_X, ALU.max))
                steps.need(m)
                v.tensor_scalar(nmax[:, a:z], rden[:, a:z], -1.0, None, ALU.mult).then_inc(z_ready, 1)

            def attend(h):
                tiles = tiles_of(h)
                a, z = tiles[0], tiles[-1] + 1
                dve.wait_ge(exp_ready, z)
                m = steps(v.reciprocal(rden[:, a:z], den[:, a:z]))
                steps.need(m)
                m = steps(v.tensor_scalar(rden[:, a:z], rden[:, a:z], tg[:, 0:1], None, ALU.mult))
                steps.need(m)
                for t in tiles:
                    m = steps(v.scalar_tensor_tensor(X[:, t, :], Z[:, t, :], rden[:, t:t + 1], X[:, t, :],
                                                     ALU.mult, ALU.add))
                steps.need(m)
                r = norm_request(tiles, [X[:, t, :] for t in tiles], 1.0, EPS)
                normalise(r, h, xn_ready)
                marks = []
                for t in tiles:
                    if h == 1:
                        dve.wait_ge(xg_ready, 2 * C * (t - 3))
                    dve.wait_ge(xn_ready, t + 1)
                    marks.append(steps(v.tensor_copy(rows16[:, t % 4, 0, :], XN[:, t, :])))
                for i, t in enumerate(tiles):
                    steps.need(marks[i])
                    m = steps(v.tensor_tensor(rows16[:, t % 4, 1, :], XN[:, t, :], rows16[:, t % 4, 0, :], ALU.subtract))
                return m

            def route(h, split_done):
                tiles = tiles_of(h)
                a, z = tiles[0], tiles[-1] + 1
                dve.wait_ge(logits_ready, h + 1)
                m = steps(v.tensor_copy(lg0[:, :, :], ps_small[:, 0:HT * E0].rearrange("p (t n) -> p t n", t=HT)))
                steps.need(m)
                for k in range(HT):
                    m = steps(v.max(top[:, k, :], lg0[:, k, :]))
                steps.need(m)
                v.tensor_scalar(nm0[:, a:z], top[:, :, 0], -1.0, None, ALU.mult).then_inc(max_ready, 1)
                for k in range(HT):
                    m = steps(v.max_index(m8i[:, k, :], top[:, k, :], lg0[:, k, :]))
                steps.need(m)
                m = steps(v.tensor_copy(idxf[:, :], m8i[:, :, 0]))
                steps.need(m)
                m = steps(v.tensor_tensor(oh[:, :, :], iota[:, None, :].to_broadcast([P, HT, E0]),
                                          idxf[:, :, None].to_broadcast([P, HT, E0]), ALU.is_equal))
                steps.need(m)
                m = steps(v.tensor_reduce(grp[:, :, :], oh[:, :, :].rearrange("p t (a b) -> p t a b", a=GR), AX_X, ALU.add))
                steps.need(m)
                steps.need(split_done)
                for t in tiles:
                    if t >= HT:
                        dve.wait_ge(xg_ready, 2 * C * (t - HT + 1))
                    for g in range(GR):
                        last = v.tensor_scalar(diag[:, t % HT, g, :], ident16[:, :], grp[:, t % HT, g:g + 1], None, ALU.mult)
                    last.then_inc(diag_ready, 1)
                dve.wait_ge(exp0_ready, h + 1)
                m = steps(v.reciprocal(wtop[:, a:z], den1[:, a:z]))
                steps.need(m)
                m = steps(v.tensor_scalar(wtop[:, a:z], wtop[:, a:z], tg[:, 2:3], None, ALU.mult))
                steps.need(m)
                m = steps(v.tensor_tensor(ohw[:, :, :], oh[:, :, :], wtop[:, a:z, None].to_broadcast([P, HT, E0]), ALU.mult))
                steps.need(m)
                steps(v.tensor_reduce(c_mem[:, a:z, :], ohw[:, :, :].rearrange("p t (a b) -> p t b a", a=GR), AX_X, ALU.add))

            ROUNDS = -(-TOPK // 8)
            FIND = 2 * ROUNDS
            found = [0]

            def find_top(t, lo, hi):
                for i in range(lo, hi):
                    if found[0]:
                        steps.need(found[0])
                    if i == 0:
                        found[0] = steps(v.tensor_copy(work[:, :], SIM[:, t, :]))
                    elif i % 2:
                        found[0] = steps(v.max(t8[:, :], work[:, :]))
                    else:
                        found[0] = steps(v.match_replace(work[:, :], t8[:, :], work[:, :], NEG))

            def adjacency(t):
                steps.need(found[0])
                dve.wait_ge(th_ready, t // HT + 1)
                k = (TOPK - 1) % 8
                v.scalar_tensor_tensor(SIM[:, t, :], SIM[:, t, :], t8[:, k:k + 1], XN[:, t, :], ALU.is_ge, ALU.mult
                                       ).then_inc(adj_ready, 1)

            def experts0(h, bp, find=None, after={}):
                FIND_AT = FIND // HT
                for k in range(HT):
                    t = HT * h + k
                    sums = Z[:, t, :]
                    dve.wait_ge(y_ready, (h * BP + bp) * HT + k + 1)
                    m = steps(v.scalar_tensor_tensor(sums, ps_y[k][:, 0:D], c_mem[:, t, 2 * bp:2 * bp + 1], sums,
                                                     ALU.mult, ALU.add))
                    if find is not None:
                        find_top(find, k * FIND_AT, k * FIND_AT + 1)
                    steps.need(m)
                    v.scalar_tensor_tensor(sums, ps_y[k][:, D:2 * D], c_mem[:, t, 2 * bp + 1:2 * bp + 2], sums,
                                           ALU.mult, ALU.add).then_inc(y_free, 1)
                    if find is not None:
                        find_top(find, k * FIND_AT + 1, (k + 1) * FIND_AT)
                    for work_behind, *args in after.get(k, ()):
                        work_behind(*args)
                if find is not None:
                    adjacency(find)

            rows_mark = [0, 0]

            def rows_sym(h, k):
                dve.wait_ge(sym_ready, 2 * h + k + 1)
                t = HT * h + 2 * k
                v.tensor_tensor(SIM[:, t:t + 2, :].rearrange("p t n -> p (t n)"),
                                SIM[:, t:t + 2, :].rearrange("p t n -> p (t n)"),
                                ps_sym[h][k][:, :], ALU.add).then_inc(sym_added, 1)

            def rows_scale(h):
                dve.wait_ge(y_free, HT + (h + 1) * BP * HT)
                dve.wait_ge(late_in, 16 * 4)
                for t in tiles_of(h):
                    rows_mark[0] = steps(v.tensor_tensor(Z[:, t, :], Z[:, t, :], scale_sb[:, :], ALU.mult))

            def rows_add(h):
                steps.need(rows_mark[0])
                for t in tiles_of(h):
                    rows_mark[0] = steps(v.tensor_tensor(X[:, t, :], X[:, t, :], Z[:, t, :], ALU.add))

            def rows_moments(h):
                steps.need(rows_mark[0])
                rows_mark[1] = norm_request(tiles_of(h), [X[:, t, :] for t in tiles_of(h)], 1.0, EPS)

            def rows_norm(h):
                r = rows_mark[1]
                dve.wait_ge(rstd_ready, r + 1)
                for k, t in enumerate(tiles_of(h)):
                    rows_mark[0] = steps(v.tensor_scalar(XN[:, t, :], X[:, t, :], mv[:, t, 0:1], rstd[:, r, k:k + 1],
                                                         ALU.subtract, ALU.mult))

            def rows_mix(h, term):
                steps.need(rows_mark[0])
                if term:
                    dve.wait_ge(sym_added, 2 * h + 2)
                for t in tiles_of(h):
                    rows_mark[0] = steps(v.scalar_tensor_tensor(X[:, t, :], (XN, SIM)[term][:, t, :],
                                                                k_mix[:, term:term + 1], X[:, t, :], ALU.mult, ALU.add))

            def top_find(h):
                for u in (2 * h, 2 * h + 1):
                    dve.wait_ge(x16hi_ready, u + 1)
                    a, z = (u % 2) * 256, (u % 2 + 1) * 256
                    v.tensor_tensor(x16[:, h, 1, :, a:z], xn_t[:, u % 2, :, :], x16[:, h, 0, :, a:z],
                                    ALU.subtract).then_inc(x16_ready, 1)
                dve.wait_ge(logits1_ready, h + 1)
                v.tensor_copy(lg[:, :, :], ps_prep[:, 0:320].rearrange("p (t n) -> p t n", t=HT)[:, :, 0:E1 + 1]
                              ).then_inc(logits1_copied, 1)
                dve.wait_ge(logits1_copied, h + 1)
                for k in range(HT):
                    m = steps(v.max(top[:, k, :], lg[:, k, 0:E1]))
                steps.need(m)
                v.tensor_scalar(nmax[:, HT * h:HT * h + HT], top[:, :, 0], -1.0, None, ALU.mult).then_inc(top_ready, 1)
                for k in range(HT):
                    top_mark[k] = steps(v.match_replace(rep[:, k, :], top[:, k, :], lg[:, k, 0:E1], NEG))

            def rows_normalise(h):
                normalise(rows_mark[1], h, xn3_ready)

            top_mark = {}

            def top_weigh(h):
                tiles = tiles_of(h)
                a, z = tiles[0], tiles[-1] + 1
                for k, t in enumerate(tiles):
                    steps.need(top_mark[k])
                    dve.wait_ge(exp1_ready, t + 1)
                    m = steps(v.scalar_tensor_tensor(ex1[:, k, :], rep[:, k, :], NEG, ex1[:, k, :],
                                                     ALU.is_equal, ALU.mult, accum_out=den[:, t:t + 1]))
                steps(v.tensor_scalar(w1[:, :, E1], sgt[:, a:z], 0.5, 0.5, ALU.mult, ALU.add))
                steps.need(m)
                m = steps(v.reciprocal(rden[:, a:z], den[:, a:z]))
                steps.need(m)
                for k, t in enumerate(tiles):
                    v.tensor_scalar(w1[:, k, 0:E1], ex1[:, k, :], rden[:, t:t + 1], None, ALU.mult
                                    ).then_inc(w1_ready, 1)

            def clear(h):
                for k in range(HT):
                    i = v.memset(Z[:, HT * h + k, :], 0.0)
                    if h == 0:
                        i.then_inc(y_free, 1)
                    else:
                        last = steps(i)
                if h == 0:
                    dve.wait_ge(y_free, HT)
                else:
                    steps.need(last)

            r0, r1 = center(0), center(1)
            normalise(r0, 0, p_ready)
            normalise(r1, 1, p_ready)
            dve.wait_ge(w0_in, 16)
            steps(v.tensor_scalar(tern[:, :, :], w0_sb, 0.25, None, ALU.is_gt))
            m = steps(v.tensor_scalar(w0_sb, w0_sb, -0.25, None, ALU.is_lt))
            steps.need(m)
            v.tensor_tensor(tern[:, :, :], tern[:, :, :], w0_sb, ALU.subtract).then_inc(tern_set, 1)
            dve.wait_ge(norm_in, 16 * 2)
            similarity(0)
            dve.wait_ge(gates_done, 1)
            steps(v.tensor_scalar(k_mix[:, 2:3], tg[:, 4:5], -0.5, 0.5, ALU.mult, ALU.add))
            m = steps(v.tensor_scalar(k_mix[:, 3:4], tg[:, 4:5], 0.125, 0.125, ALU.mult, ALU.add))
            steps.need(m)
            steps(v.tensor_tensor(k_mix[:, 0:1], k_mix[:, 2:3], tg[:, 1:2], ALU.mult))
            steps(v.tensor_tensor(k_mix[:, 1:2], k_mix[:, 3:4], tg[:, 1:2], ALU.mult))
            split_done = attend(0)
            dve.wait_ge(const_set, 4)
            clear(0)
            route(0, split_done)

            similarity(1)
            split_done = attend(1)
            experts0(0, 0)
            experts0(0, 1, find=0)
            route(1, split_done)
            experts0(0, 2, find=1)
            clear(1)
            experts0(0, 3, find=2)
            experts0(1, 0, find=3)
            experts0(1, 1, after={
                0: [(rows_scale, 0), (rows_add, 0)],
                1: [(rows_moments, 0), (rows_norm, 0), (rows_mix, 0, 0)],
                2: [(rows_sym, 0, 0), (rows_sym, 0, 1), (rows_mix, 0, 1), (rows_moments, 0)],
                3: [(rows_normalise, 0)]})
            experts0(1, 2, after={3: [(top_find, 0)]})
            experts0(1, 3, find=HT, after={1: [(top_weigh, 0)]})

            def gate_up(n, s, m=P, first=False, slot=None, loads=None):
                dve.wait_ge(up_ready, n + 1)
                dve.wait_ge(silu_ready, n + 1)
                v.tensor_tensor(gated[0:m, s, :], silu[0:m, s, :], ps_up[s][0:m, :], ALU.mult).then_inc(gated_ready, 1)
                if slot is None:
                    slot, loads = n % WS, n // WS + 1
                dve.wait_ge(w_in[slot], loads * 32)
                dve.wait_ge(gated_ready, n + 1)
                if not first:
                    dve.wait_ge(ihi_ready, n - 1)
                v.tensor_tensor(inter[0:m, s, :], gated[0:m, s, :], w_rows[0:m, slot, :], ALU.mult).then_inc(inter_ready, 1)

            def low_step(n, s, m=P):
                dve.wait_ge(inter_ready, n + 1)
                dve.wait_ge(ihi_ready, n + 1)
                v.tensor_tensor(inter16[0:m, s, 1, :], inter[0:m, s, :], inter16[0:m, s, 0, :], ALU.subtract
                                ).then_inc(ilo_ready, 1)

            def final(h):
                dve.wait_ge(down_ready, (h + 1) * NS)
                for k in range(HT):
                    t = HT * h + k
                    v.scalar_tensor_tensor(X[:, t, :], ps_down[k // 2][:, (k % 2) * D:(k % 2 + 1) * D], tg[:, 3:4],
                                           X[:, t, :], ALU.mult, ALU.add).then_inc(out_ready, 1)

            for n in range(NS):
                q, s, m = n - 1, (n + 1) % 2, I1 if n == 0 else P
                gate_up(n, s, m, first=(n < 2))
                t, i = HT + 1 + (q - 1) // 5, (q - 1) % 5 * 4
                finding = 1 <= q <= 5 * (HT - 1)
                if finding:
                    find_top(t, i, i + 2)
                if q == 16:
                    rows_sym(1, 0)
                if q == 17:
                    rows_scale(1)
                if q == 18:
                    rows_sym(1, 1)
                if q == 19:
                    rows_add(1)
                if q == 20:
                    rows_moments(1)
                if q == 21:
                    rows_norm(1)
                if q == 22:
                    rows_mix(1, 0)
                if q == 23:
                    rows_mix(1, 1)
                if q == 24:
                    rows_moments(1)
                if q == 25:
                    rows_normalise(1)
                if q == 28:
                    top_find(1)
                if q == 29:
                    top_weigh(1)
                low_step(n, s, m)
                if finding:
                    find_top(t, i + 2, i + 4)
                    if q % 5 == 0:
                        adjacency(t)
            gate_up(NS, 0, I1)
            low_step(NS, 0, I1)
            gate_up(NS + 1, 1)
            final(0)
            low_step(NS + 1, 1)
            with dve.Fori(0, (NS - WS + 1) // WS) as turn:
                for j in range(WS):
                    n0 = NS + 2 + j
                    gate_up(turn * WS + n0, j % 2, slot=n0 % WS, loads=turn + (n0 // WS + 1))
                    low_step(turn * WS + n0, j % 2)
            for n in range(2 * NS - 3, 2 * NS):
                gate_up(n, (n + 1) % 2)
                low_step(n, (n + 1) % 2)
            final(1)


def kernel(**inputs):
    import numpy as np
    import concourse.bacc as bacc
    from concourse.bass_utils import run_bass_kernel_spmd

    a = {k: np.asarray(w) for k, w in inputs.items()}
    laid = {
        "x": a["x"],
        "ctx_t": a["ctx_512"].reshape(B * S, DC).T,
        "g_xattn": a["g_xattn"], "g_ffn": a["g_ffn"],
        "wk_t": a["L0_xattn_W_k"].T, "b_k": a["L0_xattn_b_k"],
        "ln_gamma": a["L0_xattn_ln_gamma"], "ln_beta": a["L0_xattn_ln_beta"],
        "w0_t": a["L0_ffn_weight"].T, "scale0": a["L0_ffn_scale"],
        "masks_t": a["L0_ffn_expert_masks"].transpose(2, 0, 1).reshape(D, E0 // 2, 2 * D),
        "router_t": a["L0_ffn_router_w"].T,
        "wq1_t": a["L1_xattn_Wq"].T, "wk1_t": a["L1_xattn_Wk"].T,
        "gamma_raw": a["L1_xattn_gamma_raw"].reshape(1),
        "gate_t": a["L1_ffn_gate_w"].T,
        "gu_t": a["L1_ffn_gu_w"].reshape(PAIRS, 2, 2, I1, D).transpose(4, 0, 2, 1, 3).reshape(D, PAIRS, 4 * I1),
        "dp_t": a["L1_ffn_dp_w"].transpose(0, 2, 1).reshape(E1 * I1, D),
        "shg_t": a["L1_ffn_sh_gate_w"].T, "shu_t": a["L1_ffn_sh_up_w"].T,
        "shd_t": a["L1_ffn_sh_down_w"].T, "shgate_t": a["L1_ffn_sh_gate1_w"].T,
    }
    nc = bacc.Bacc("TRN2", target_bir_lowering=False, num_devices=1)
    arrays, args = {}, []
    for name, w in laid.items():
        w = np.ascontiguousarray(w)
        arrays[f"in_{name}"] = w
        args.append(nc.dram_tensor(f"in_{name}", w.shape, mybir.dt.from_np(w.dtype), kind="ExternalInput").ap())
    out = nc.dram_tensor("out", (B, S, D), F32, kind="ExternalOutput").ap()
    flamingo_block(nc, *args, out)
    r = run_bass_kernel_spmd(nc, [arrays], core_ids=[0])
    return r.results[0]["out"]
```
